# Optimizing a Trainium2 kernel written in Bass

```python
import numpy as np
import jax
import jax.numpy as jnp

def _softmax(x, axis=-1):
    return jax.nn.softmax(x, axis=axis)

def _gelu(x):
    return jax.nn.gelu(x, approximate=True)

def _silu(x):
    return jax.nn.silu(x)

def _sigmoid(x):
    return jax.nn.sigmoid(x)

def _layernorm(x, axis=-1, eps=1e-05):
    m = jnp.mean(x, axis=axis, keepdims=True)
    v = jnp.var(x, axis=axis, keepdims=True)
    return (x - m) / jnp.sqrt(v + eps)

def _scatter_add(tgt, idx, src, axis=0):
    return tgt.at[idx].add(src)

def _segment_sum(src, seg, n):
    return jax.ops.segment_sum(src, seg, n)
kernel_name = 'mk_macaron_d1_jaxref_r4_72aa84'

def setup_inputs(seed: int=0):
    np.random.seed(seed)
    _w = jnp.asarray

    def _L0_attn_setup():
        import jax, jax.numpy as jnp
        import numpy as np
        B, S, D = (2, 512, 512)
        N_HEADS, N_KV_HEADS = (16, 4)
        HEAD_DIM = D // N_HEADS

        def _apply_rope(xh, positions):
            Dh = xh.shape[-1]
            half = Dh // 2
            freqs = 1.0 / 10000.0 ** (jnp.arange(half, dtype=jnp.float32) / half)
            angles = positions[:, None].astype(jnp.float32) * freqs[None, :]
            cos, sin = (jnp.cos(angles), jnp.sin(angles))
            xp = xh.reshape(*xh.shape[:-1], half, 2)
            x0, x1 = (xp[..., 0], xp[..., 1])
            r0 = x0 * cos - x1 * sin
            r1 = x0 * sin + x1 * cos
            return jnp.stack([r0, r1], axis=-1).reshape(xh.shape)
        key = jax.random.key(seed)
        ks = jax.random.split(key, 5)
        x = jax.random.normal(ks[0], (B, S, D), dtype=jnp.float32)
        W_q = jax.random.normal(ks[1], (D, D), dtype=jnp.float32) * 0.02
        W_k = jax.random.normal(ks[2], (D, N_KV_HEADS * HEAD_DIM), dtype=jnp.float32) * 0.02
        W_v = jax.random.normal(ks[3], (D, N_KV_HEADS * HEAD_DIM), dtype=jnp.float32) * 0.02
        W_o = jax.random.normal(ks[4], (D, D), dtype=jnp.float32) * 0.02
        return {'x': x, 'W_q': W_q, 'W_k': W_k, 'W_v': W_v, 'W_o': W_o}
    _L0_attn_in = _L0_attn_setup()

    def _L0_ffn_setup():
        import jax, jax.numpy as jnp
        import numpy as np

        def _sparsify_2to4(h):
            B, S, I = h.shape
            g = h.reshape(B, S, I // 4, 4)
            a = jnp.abs(g)
            _, idx = jax.lax.top_k(a, 2)
            pos = jnp.arange(4)
            mask = (pos == idx[..., 0:1]) | (pos == idx[..., 1:2])
            return (g * mask.astype(g.dtype)).reshape(B, S, I)
        key = jax.random.key(seed)
        k1, k2, k3, k4 = jax.random.split(key, 4)
        B, S, H, I = (4, 512, 512, 2048)
        x = jax.random.normal(k1, (B, S, H), dtype=jnp.float32)
        w_gate = jax.random.normal(k2, (H, I), dtype=jnp.float32) / np.sqrt(H)
        w_up = jax.random.normal(k3, (H, I), dtype=jnp.float32) / np.sqrt(H)
        w_down = jax.random.normal(k4, (I, H), dtype=jnp.float32) / np.sqrt(I)
        return {'x': x, 'w_gate': w_gate, 'w_up': w_up, 'w_down': w_down}
    _L0_ffn_in = _L0_ffn_setup()
    _d = {'L0_attn_x': _L0_attn_in['x'], 'L0_attn_W_q': _L0_attn_in['W_q'], 'L0_attn_W_k': _L0_attn_in['W_k'], 'L0_attn_W_v': _L0_attn_in['W_v'], 'L0_attn_W_o': _L0_attn_in['W_o'], 'L0_ffn_w_gate': _L0_ffn_in['w_gate'], 'L0_ffn_w_up': _L0_ffn_in['w_up'], 'L0_ffn_w_down': _L0_ffn_in['w_down']}
    _x0 = _d['L0_attn_x']
    _d['L0_attn_x'] = jax.random.normal(jax.random.fold_in(jax.random.key(seed), 1), (8, 512, 512), dtype=_x0.dtype)
    del _x0
    return _d

def reference(L0_attn_x, L0_attn_W_q, L0_attn_W_k, L0_attn_W_v, L0_attn_W_o, L0_ffn_w_gate, L0_ffn_w_up, L0_ffn_w_down):

    def _L0_attn_ref(x, W_q, W_k, W_v, W_o):
        import jax, jax.numpy as jnp
        import numpy as np
        B, S, D = (2, 512, 512)
        N_HEADS, N_KV_HEADS = (16, 4)
        HEAD_DIM = D // N_HEADS

        def _apply_rope(xh, positions):
            Dh = xh.shape[-1]
            half = Dh // 2
            freqs = 1.0 / 10000.0 ** (jnp.arange(half, dtype=jnp.float32) / half)
            angles = positions[:, None].astype(jnp.float32) * freqs[None, :]
            cos, sin = (jnp.cos(angles), jnp.sin(angles))
            xp = xh.reshape(*xh.shape[:-1], half, 2)
            x0, x1 = (xp[..., 0], xp[..., 1])
            r0 = x0 * cos - x1 * sin
            r1 = x0 * sin + x1 * cos
            return jnp.stack([r0, r1], axis=-1).reshape(xh.shape)
        b, s, d = x.shape
        positions = jnp.arange(s)
        rep = N_HEADS // N_KV_HEADS
        Q = (x @ W_q).reshape(b, s, N_HEADS, HEAD_DIM).transpose(0, 2, 1, 3)
        K = (x @ W_k).reshape(b, s, N_KV_HEADS, HEAD_DIM).transpose(0, 2, 1, 3)
        V = (x @ W_v).reshape(b, s, N_KV_HEADS, HEAD_DIM).transpose(0, 2, 1, 3)
        Qr = _apply_rope(Q, positions)
        K_rep = jnp.tile(K, (1, rep, 1, 1))
        V_rep = jnp.tile(V, (1, rep, 1, 1))
        Kr = _apply_rope(K_rep, positions)
        scores = jnp.einsum('bhqd,bhkd->bhqk', Qr, Kr) / HEAD_DIM ** 0.5
        weights = jax.nn.softmax(scores, axis=-1)
        out = jnp.einsum('bhqk,bhkd->bhqd', weights, V_rep)
        out = out.transpose(0, 2, 1, 3).reshape(b, s, d)
        return out @ W_o

    def _L0_ffn_ref(x, w_gate, w_up, w_down):
        import jax, jax.numpy as jnp
        import numpy as np

        def _sparsify_2to4(h):
            B, S, I = h.shape
            g = h.reshape(B, S, I // 4, 4)
            a = jnp.abs(g)
            _, idx = jax.lax.top_k(a, 2)
            pos = jnp.arange(4)
            mask = (pos == idx[..., 0:1]) | (pos == idx[..., 1:2])
            return (g * mask.astype(g.dtype)).reshape(B, S, I)
        h = jax.nn.silu(jnp.einsum('bsh,hi->bsi', x, w_gate)) * jnp.einsum('bsh,hi->bsi', x, w_up)
        h_sparse = _sparsify_2to4(h)
        return jnp.einsum('bsi,ih->bsh', h_sparse, w_down)
    x = L0_attn_x
    x = x + 0.5 * _L0_ffn_ref(_layernorm(x, axis=-1), L0_ffn_w_gate, L0_ffn_w_up, L0_ffn_w_down)
    x = x + _L0_attn_ref(_layernorm(x, axis=-1), L0_attn_W_q, L0_attn_W_k, L0_attn_W_v, L0_attn_W_o)
    x = x + 0.5 * _L0_ffn_ref(_layernorm(x, axis=-1), L0_ffn_w_gate, L0_ffn_w_up, L0_ffn_w_down)
    return x

_drawn_inputs = setup_inputs


def setup_inputs(seed=0):
    import zlib

    import numpy as np

    out = dict(_drawn_inputs(seed))
    spreads = {}
    factors = {'L0_attn_W_q': 8.0, 'L0_attn_W_k': 8.0, 'L0_attn_W_v': 5.002, 'L0_attn_W_o': 5.093}
    for name, (base, spread) in spreads.items():
        noise = np.random.default_rng([zlib.crc32(name.encode()), seed]).standard_normal(out[name].shape)
        drawn = base * np.exp(spread * noise) if base else spread * noise
        out[name] = jnp.asarray(drawn.astype(out[name].dtype))
    for name, factor in factors.items():
        out[name] = (out[name] * factor).astype(out[name].dtype)
    return out
```

```python
from contextlib import ExitStack

import numpy as np

import concourse.bass as bass
from concourse import mybir

FP32 = mybir.dt.float32
FP32R = mybir.dt.float32r
BF16 = mybir.dt.bfloat16
ALU = mybir.AluOpType
ACT = mybir.ActivationFunctionType
AX = mybir.AxisListType

P = 128
N = 512
EPS = 1e-5
HEAD = 32


def ffn_phase(nc, ident_dram, x_in, x_out, w_gate, w_up, w_down, tag):
    TOKENS, H = x_in.shape
    I = w_gate.shape[1]
    KC = H // P
    SUB = N // P
    GROUP = 2 * N
    GROUPS = TOKENS // GROUP
    BLOCKS = I // N
    R = 4
    UNITS = 2 * BLOCKS
    QUARTERS = 6
    STEPS = 10

    ctx = ExitStack()
    with ctx:
        def sb(name, shape, dtype=FP32):
            return ctx.enter_context(nc.sbuf_tensor(f"{tag}_{name}", shape, dtype))

        def sem(name):
            return ctx.enter_context(nc.semaphore(f"{tag}_{name}"))

        w_hi = sb("w_hi", [P, 2, 3, R * N], FP32R)
        w_lo = sb("w_lo", [P, 2, 3, R * N], FP32R)
        stage = sb("stage", [P, 2, 2, N])
        xt_hi = sb("xt_hi", [P, KC, GROUP], FP32R)
        xt_lo = sb("xt_lo", [P, KC, GROUP], FP32R)
        xn = sb("xn", [P, SUB, H])
        acc = sb("acc", [P, 2, SUB, H])
        h = sb("h", [P, R, N])
        hs_hi = sb("hs_hi", [P, R, N], FP32R)
        hs_lo = sb("hs_lo", [P, R, N], FP32R)
        mag = sb("mag", [P, R, N])
        top = sb("top", [P, 2, N])
        first = sb("first", [P, 2, N], BF16)
        both = sb("both", [P, 2, N], BF16)
        split = sb("split", [P, 2, N], BF16)
        keep = sb("keep", [P, R, N], BF16)
        ident = sb("ident", [P, P])
        stats = sb("stats", [P, SUB, 6])
        moments = sb("moments", [P, SUB, 2])
        shifted = sb("shifted", [P, SUB])
        rstd = sb("rstd", [P, SUB])
        power = sb("power", [P, SUB])
        eps = sb("eps", [P, SUB])

        gu = ctx.enter_context(nc.psum_tensor(f"{tag}_gu", [P, 2, 2, N], FP32))
        y = ctx.enter_context(nc.psum_tensor(f"{tag}_y", [P, SUB, H], FP32))

        ident_loaded = sem("ident_loaded")
        stage_loaded = [sem("stage_loaded0"), sem("stage_loaded1")]
        xn_loaded = sem("xn_loaded")
        acc_loaded = [sem("acc_loaded0"), sem("acc_loaded1")]
        acc_stored = [sem("acc_stored0"), sem("acc_stored1")]
        w_hi_done = sem("w_hi_done")
        w_lo_done = sem("w_lo_done")
        stats_done = sem("stats_done")
        power_set = sem("power_set")
        shift_done = sem("shift_done")
        rstd_done = sem("rstd_done")
        xn_done = sem("xn_done")
        xt_turned = sem("xt_turned")
        xt_hi_done = sem("xt_hi_done")
        xt_lo_done = sem("xt_lo_done")
        gu_done = sem("gu_done")
        silu_done = sem("silu_done")
        h_done = sem("h_done")
        mag_done = sem("mag_done")
        mask_step = sem("mask_step")
        masked = sem("masked")
        hs_hi_done = sem("hs_hi_done")
        hs_lo_done = sem("hs_lo_done")
        down_done = sem("down_done")
        y_added = sem("y_added")

        even, odd = mag[:, 0:R:2, :], mag[:, 1:R:2, :]
        def pieces(u):
            b, half = u // 2, u % 2
            start = b * QUARTERS + (0 if half == 0 else 2)
            gaps = (0, 1) if half == 0 else (0, 1, 2, 2)
            return [(g, start + k) for k, g in enumerate(gaps)]

        def piece_views(q, b):
            kind, part = q // 2, q % 2
            w = [w_hi[:, b, kind, :], w_lo[:, b, kind, :]]
            if kind < 2:
                dst = [v.rearrange("p (k r c) -> p k r c", k=KC, r=R)[:, 2 * part:2 * part + 2] for v in w]
                return dst, lambda s: s.rearrange("p k (c r) -> p k r c", r=R)
            dst = [v.rearrange("p (r n) -> p r n", r=R)[:, 2 * part:2 * part + 2, :] for v in w]
            return dst, lambda s: s

        def last_units(last):
            return UNITS - 2 if last else UNITS

        def loop(eng, body):
            body(0, True, False)
            if GROUPS > 2:
                with eng.Fori(1, GROUPS - 1) as g:
                    body(g, False, False)
            body(GROUPS - 1, False, True)

        block = ctx.enter_context(nc.Block())

        @block.sync
        def _(sync):
            def load_piece(g, n):
                block_of, q = n // QUARTERS % BLOCKS, n % QUARTERS
                kind, part = q // 2, q % 2
                count = g * (BLOCKS * QUARTERS) + n
                if n >= 2:
                    sync.wait_ge(w_lo_done, count - 1)
                if kind < 2:
                    src = (w_gate, w_up)[kind].rearrange("(k p) i -> p k i", p=P)
                    src = src[:, 2 * part:2 * part + 2, block_of * N:(block_of + 1) * N]
                else:
                    src = w_down.rearrange("(b p r) n -> b p r n", p=P, r=R)[block_of, :, 2 * part:2 * part + 2, :]
                sync.dma_start(stage[:, n % 2], src).then_inc(stage_loaded[n % 2], 16)

            def rows(g, half):
                return bass.ds(g * GROUP + half * N, N)

            def tiles(dram, g, half):
                return dram[rows(g, half), :].rearrange("(t p) n -> p t n", p=P)

            def store(g, half):
                sync.wait_ge(y_added, (g * UNITS + UNITS - 1 + half) * SUB)
                sync.dma_start(tiles(x_out, g, half), acc[:, half]).then_inc(acc_stored[half], 16)

            def reload(g, half):
                sync.wait_ge(acc_stored[half], g * 16)
                sync.dma_start(acc[:, half], tiles(x_in, g, half)).then_inc(acc_loaded[half], 16)

            sync.dma_start(xn[:], tiles(x_in, 0, 0)).then_inc(xn_loaded, 16)
            sync.dma_start(ident[:], ident_dram).then_inc(ident_loaded, 16)
            for n in range(4):
                load_piece(0, n)
            sync.wait_ge(xt_turned, SUB)
            sync.dma_start(xn[:], tiles(x_in, 0, 1)).then_inc(xn_loaded, 16)
            for n in range(4, QUARTERS):
                load_piece(0, n)
            for half in range(2):
                sync.dma_start(acc[:, half], tiles(x_in, 0, half)).then_inc(acc_loaded[half], 16)
            for n in range(2):
                load_piece(0, QUARTERS + n)

            def body(g, first, last):
                end = QUARTERS * (BLOCKS - 1) if last else QUARTERS * BLOCKS + 2
                for u in range(UNITS):
                    for _, c in pieces(u):
                        if c + 2 < end:
                            load_piece(g, QUARTERS + c + 2)
                    if u == 0 and not first:
                        store(g - 1, 1)
                        reload(g, 1)
                    if u == UNITS - 3 and not last:
                        sync.wait_ge(xt_turned, g * 2 * SUB + 2 * SUB)
                        sync.dma_start(xn[:], tiles(x_in, g + 1, 0)).then_inc(xn_loaded, 16)
                if not last:
                    sync.wait_ge(xt_turned, g * 2 * SUB + 3 * SUB)
                    sync.dma_start(xn[:], tiles(x_in, g + 1, 1)).then_inc(xn_loaded, 16)
                store(g, 0)
                if not last:
                    reload(g + 1, 0)

            loop(sync, body)
            store(GROUPS - 1, 1)
            for half in range(2):
                sync.wait_ge(acc_stored[half], GROUPS * 16)

        @block.gpsimd
        def _(pool):
            pool.memset(power[:], -0.5).then_inc(power_set, 1)
            pool.memset(eps[:], EPS).then_inc(power_set, 1)
            pool.wait_ge(power_set, 2)
            with pool.Fori(0, 2 * GROUPS) as i:
                pool.wait_ge(stats_done, (i + 1) * SUB)
                pool.tensor_tensor(shifted[:], moments[:, :, 1], eps[:], ALU.add).then_inc(shift_done, 1)
                pool.wait_ge(shift_done, i + 1)
                pool.tensor_tensor(rstd[:], shifted[:], power[:], ALU.pow).then_inc(rstd_done, 1)

        @block.scalar
        def _(act):
            def split_piece(g, n):
                q, b = n % QUARTERS, n // QUARTERS % 2
                count = g * (BLOCKS * QUARTERS) + n
                act.wait_ge(stage_loaded[n % 2], (g * (BLOCKS * QUARTERS // 2) + n // 2 + 1) * 16)
                dst, view = piece_views(q, b)
                act.activation(dst[0], view(stage[:, n % 2]), ACT.Copy).then_inc(w_hi_done, 1)

            def tile_hi(count, half, t):
                act.wait_ge(xt_turned, count + 1)
                at = half * N + t * P
                act.activation(xt_hi[:, :, at:at + P], gu[:, t // 2, t % 2, :].rearrange("p (k c) -> p k c", k=KC),
                               ACT.Copy).then_inc(xt_hi_done, 1)

            for n in range(2):
                split_piece(0, n)
            for t in range(SUB):
                tile_hi(t, 0, t)
            for n in range(2, 4):
                split_piece(0, n)

            def body(g, first, last):
                for u in range(UNITS):
                    unit = g * UNITS + u
                    splits = pieces(u) if u < last_units(last) else []
                    for r in range(R):
                        act.wait_ge(gu_done, unit * R + r + 1)
                        if not (first and u == 0):
                            act.wait_ge(hs_lo_done, unit * R - R + r + 1)
                        act.activation(h[:, r, :], gu[:, r % 2, 0, :], ACT.Silu).then_inc(silu_done, 1)
                        if first and u == 0 and r == 0:
                            for n in range(4, QUARTERS):
                                split_piece(0, n)
                        for gap, c in splits:
                            if gap == r:
                                if not (first and u < 2):
                                    act.wait_ge(gu_done if c % QUARTERS < 4 else down_done, (g * UNITS + u - u % 2) * R)
                                split_piece(g, QUARTERS + c)
                        if r >= 2:
                            pair = r - 2
                            act.wait_ge(h_done, unit * R + 2 * pair + 2)
                            act.activation(mag[:, 2 * pair:2 * pair + 2, :], h[:, 2 * pair:2 * pair + 2, :],
                                           ACT.Abs).then_inc(mag_done, 1)
                    if u == 0:
                        for t in range(SUB):
                            tile_hi(g * 2 * SUB + SUB + t, 1, t)
                    if u == UNITS - 1 and not last:
                        for t in range(SUB):
                            tile_hi(g * 2 * SUB + 2 * SUB + t, 0, t)
                    for r in range(R):
                        act.wait_ge(masked, unit * R + r + 1)
                        if not (first and u == 0):
                            act.wait_ge(down_done, unit * R - R + r + 1)
                        act.activation(hs_hi[:, r, :], h[:, r, :], ACT.Copy).then_inc(hs_hi_done, 1)

            loop(act, body)

        @block.vector
        def _(dve):
            def split_piece(g, n):
                q, b = n % QUARTERS, n // QUARTERS % 2
                dst, view = piece_views(q, b)
                dve.wait_ge(w_hi_done, g * (BLOCKS * QUARTERS) + n + 1)
                dve.tensor_tensor(dst[1], view(stage[:, n % 2]), dst[0].bitcast(FP32),
                                  ALU.subtract).then_inc(w_lo_done, 1)

            def tile_lo(count, half, t):
                dve.wait_ge(xt_hi_done, count + 1)
                at = half * N + t * P
                dve.tensor_tensor(xt_lo[:, :, at:at + P], gu[:, t // 2, t % 2, :].rearrange("p (k c) -> p k c", k=KC),
                                  xt_hi[:, :, at:at + P].bitcast(FP32), ALU.subtract).then_inc(xt_lo_done, 1)

            def tile_stats(k):
                dve.wait_ge(xn_loaded, (k + 1) * 16)
                for t in range(SUB):
                    dve.bn_stats(stats[:, t, :], xn[:, t, :])
                dve.drain()
                for t in range(SUB):
                    dve.bn_aggr(moments[:, t, :], stats[:, t, :]).then_inc(stats_done, 1)

            def tile_norm(k):
                dve.wait_ge(rstd_done, k + 1)
                for t in range(SUB):
                    dve.tensor_scalar(xn[:, t, :], xn[:, t, :], moments[:, t, 0:1], rstd[:, t:t + 1],
                                      ALU.subtract, ALU.mult).then_inc(xn_done, 1)

            def add_block(g, u):
                half = u % 2
                dve.wait_ge(down_done, (g * UNITS + u + 1) * R)
                if u < 2:
                    dve.wait_ge(acc_loaded[half], (g + 1) * 16)
                else:
                    dve.wait_ge(y_added, (g * UNITS + u - 1) * SUB)
                for t in range(SUB):
                    dve.scalar_tensor_tensor(acc[:, half, t, :], y[:, t, :], 0.5, acc[:, half, t, :],
                                             ALU.mult, ALU.add).then_inc(y_added, 1)

            def choose(unit):
                step = unit * STEPS
                dve.wait_ge(mag_done, unit * 2 + 2)
                dve.tensor_tensor(first[:], even, odd, ALU.is_ge).then_inc(mask_step, 1)
                dve.tensor_tensor(top[:], even, odd, ALU.max).then_inc(mask_step, 1)
                dve.wait_ge(mask_step, step + 2)
                dve.tensor_tensor(even, even, odd, ALU.min).then_inc(mask_step, 1)
                dve.wait_ge(mask_step, step + 3)
                dve.tensor_tensor(both[:, 0, :], mag[:, 0, :], top[:, 1, :], ALU.is_ge).then_inc(mask_step, 1)
                dve.tensor_tensor(both[:, 1, :], mag[:, 2, :], top[:, 0, :], ALU.is_gt).then_inc(mask_step, 1)
                dve.wait_ge(mask_step, step + 5)
                dve.tensor_scalar(split[:, 0, :], both[:, 1, :], -1.0, 1.0, ALU.mult, ALU.add).then_inc(mask_step, 1)
                dve.tensor_scalar(split[:, 1, :], both[:, 0, :], -1.0, 1.0, ALU.mult, ALU.add).then_inc(mask_step, 1)
                dve.wait_ge(mask_step, step + 7)
                dve.tensor_tensor(keep[:, 0:R:2, :], first[:], split[:], ALU.mult).then_inc(mask_step, 1)
                dve.wait_ge(mask_step, step + 8)
                dve.tensor_tensor(keep[:, 1:R:2, :], split[:], keep[:, 0:R:2, :], ALU.subtract).then_inc(mask_step, 1)
                dve.wait_ge(mask_step, step + 9)
                pairs = keep[:].rearrange("p (a e) n -> p a e n", e=2)
                dve.tensor_tensor(pairs, pairs, both[:].unsqueeze(2).broadcast_to((P, 2, 2, N)),
                                  ALU.max).then_inc(mask_step, 1)

            def apply(unit):
                dve.wait_ge(mask_step, unit * STEPS + STEPS)
                for r in range(R):
                    dve.tensor_tensor(h[:, r, :], h[:, r, :], keep[:, r, :], ALU.mult).then_inc(masked, 1)
                for r in range(R):
                    dve.wait_ge(hs_hi_done, unit * R + r + 1)
                    dve.tensor_tensor(hs_lo[:, r, :], h[:, r, :], hs_hi[:, r, :].bitcast(FP32),
                                      ALU.subtract).then_inc(hs_lo_done, 1)

            tile_stats(0)
            for n in range(2):
                split_piece(0, n)
            tile_norm(0)
            for t in range(SUB):
                tile_lo(t, 0, t)
            for n in range(2, 4):
                split_piece(0, n)

            def body(g, first, last):
                for u in range(UNITS):
                    unit = g * UNITS + u
                    splits = pieces(u) if u < last_units(last) else []
                    for r in range(R):
                        dve.wait_ge(silu_done, unit * R + r + 1)
                        dve.tensor_tensor(h[:, r, :], h[:, r, :], gu[:, r % 2, 1, :], ALU.mult).then_inc(h_done, 1)
                        if first and u == 0 and r == 0:
                            for n in range(4, QUARTERS):
                                split_piece(0, n)
                        for gap, c in splits:
                            if gap == r:
                                split_piece(g, QUARTERS + c)
                        if u == 0 and r == 0:
                            tile_stats(2 * g + 1)
                        if u == 0 and r == 1:
                            tile_norm(2 * g + 1)
                        if u == UNITS - 2 and r == 2 and not last:
                            tile_stats(2 * g + 2)
                        if u == UNITS - 1 and r == 1 and not last:
                            tile_norm(2 * g + 2)
                    choose(unit)
                    if u == 0:
                        for t in range(SUB):
                            tile_lo(g * 2 * SUB + SUB + t, 1, t)
                    if u == UNITS - 1 and not last:
                        for t in range(SUB):
                            tile_lo(g * 2 * SUB + 2 * SUB + t, 0, t)
                    apply(unit)
                    if u:
                        add_block(g, u - 1)
                    elif not first:
                        add_block(g - 1, UNITS - 1)

            loop(dve, body)
            add_block(GROUPS - 1, UNITS - 1)

        @block.tensor
        def _(pe):
            def gate_up(g, u, r, first):
                unit, b = g * UNITS + u, u // 2 % 2
                half = u % 2
                if r == 0:
                    if u < 2:
                        pe.wait_ge(xt_lo_done, g * 2 * SUB + (u + 1) * SUB)
                    if half == 0:
                        pe.wait_ge(w_lo_done, g * (BLOCKS * QUARTERS) + u // 2 * QUARTERS + 4)
                if not (first and u == 0 and r < 2):
                    pe.wait_ge(h_done, unit * R + r - 1)
                for kind in range(2):
                    whi = w_hi[:, b, kind, :].rearrange("p (k r c) -> p k r c", k=KC, r=R)
                    wlo = w_lo[:, b, kind, :].rearrange("p (k r c) -> p k r c", k=KC, r=R)
                    for k in range(KC):
                        xh = xt_hi[:, k, half * N:(half + 1) * N]
                        xl = xt_lo[:, k, half * N:(half + 1) * N]
                        for i, (w, x) in enumerate(((whi, xh), (whi, xl), (wlo, xh))):
                            last = nc.tensor.matmul(gu[:, r % 2, kind, :], w[:, k, r, :], x,
                                                    start=k == 0 and i == 0, stop=k == KC - 1 and i == 2)
                last.then_inc(gu_done, 1)

            def down(g, u, turned=None):
                unit, b = g * UNITS + u, u // 2 % 2
                if not (isinstance(unit, int) and unit == 0):
                    pe.wait_ge(y_added, unit * SUB)
                if u % 2 == 0:
                    pe.wait_ge(w_lo_done, g * (BLOCKS * QUARTERS) + u // 2 * QUARTERS + 6)
                for r in range(R):
                    if r == R // 2 and turned is not None:
                        turn_half(turned, unit + 1)
                    pe.wait_ge(hs_lo_done, unit * R + r + 1)
                    wh = w_hi[:, b, 2, r * N:(r + 1) * N]
                    wl = w_lo[:, b, 2, r * N:(r + 1) * N]
                    for t in range(SUB):
                        at = slice(t * P, (t + 1) * P)
                        for i, (x, w) in enumerate(((hs_hi, wh), (hs_hi, wl), (hs_lo, wh))):
                            last = nc.tensor.matmul(y[:, t, :], x[:, r, at], w, start=r == 0 and i == 0,
                                                    stop=r == R - 1 and i == 2)
                    last.then_inc(down_done, 1)

            def turn(count, t):
                pe.wait_ge(xn_done, count + 1)
                for k in range(KC):
                    last = nc.tensor.transpose(gu[:, t // 2, t % 2, k * P:(k + 1) * P], xn[:, t, k * P:(k + 1) * P],
                                               ident[:])
                last.then_inc(xt_turned, 1)

            def turn_half(count, unit):
                pe.wait_ge(h_done, (unit + 1) * R)
                for t in range(SUB):
                    turn(count + t, t)

            pe.wait_ge(ident_loaded, 16)
            for t in range(SUB):
                turn(t, t)

            def body(g, first, last):
                for u in range(UNITS):
                    for r in range(R):
                        gate_up(g, u, r, first)
                    if u == 0:
                        second = g * 2 * SUB + SUB
                        if first:
                            turn_half(second, g * UNITS)
                        else:
                            down(g - 1, UNITS - 1, second)
                    elif u == UNITS - 1 and not last:
                        down(g, u - 1, g * 2 * SUB + 2 * SUB)
                    else:
                        down(g, u - 1)

            loop(pe, body)
            down(GROUPS - 1, UNITS - 1)


def qkv_phase(nc, ident_dram, cos_dram, sin_dram, x_in, w_q, w_k, w_v, qk_hi_out, qk_lo_out, v_out, seq):
    TOKENS, H = x_in.shape
    KC = H // P
    TILES = seq // P
    SEQS = TOKENS // seq
    DQ, DK = w_q.shape[1], w_k.shape[1]
    QK = DQ + DK
    ALL = QK + DK
    CH = QK // P
    KVH = DK // HEAD

    ctx = ExitStack()
    with ctx:
        def sb(name, shape, dtype=FP32):
            return ctx.enter_context(nc.sbuf_tensor(f"qkv_{name}", shape, dtype))

        def ps(name, shape):
            return ctx.enter_context(nc.psum_tensor(f"qkv_{name}", shape, FP32))

        def sem(name):
            return ctx.enter_context(nc.semaphore(f"qkv_{name}"))

        w = sb("w", [P, KC, ALL])
        w_hi = sb("w_hi", [P, KC, ALL], FP32R)
        w_lo = sb("w_lo", [P, KC, ALL], FP32R)
        cos = sb("cos", [P, TILES, QK])
        sin = sb("sin", [P, TILES, QK])
        ident = sb("ident", [P, P])
        x = sb("x", [P, TILES, H])
        xn = sb("xn", [P, TILES, H])
        xt_hi = sb("xt_hi", [P, 2, KC, P], FP32R)
        xt_lo = sb("xt_lo", [P, 2, KC, P], FP32R)
        rot = sb("rot", [P, 2, QK])
        cross = sb("cross", [P, QK])
        qk_hi = sb("qk_hi", [P, CH, seq], FP32R)
        qk_lo = sb("qk_lo", [P, CH, seq], FP32R)
        v = sb("v", [P, TILES, KVH * P], FP32R)
        stats = sb("stats", [P, TILES, 6])
        moments = sb("moments", [P, TILES, 2])
        shifted = sb("shifted", [P, TILES])
        rstd = sb("rstd", [P, TILES])
        power = sb("power", [P, TILES])
        eps = sb("eps", [P, TILES])

        xbank = ps("xbank", [P, 2, KC * P])
        proj = ps("proj", [P, 2, 2 * N])
        qbank = ps("qbank", [P, 2 * N])

        const_loaded = sem("const_loaded")
        w_loaded = sem("w_loaded")
        x_loaded = sem("x_loaded")
        w_hi_done = sem("w_hi_done")
        w_lo_done = sem("w_lo_done")
        v_cleared = sem("v_cleared")
        stats_done = sem("stats_done")
        power_set = sem("power_set")
        shift_done = sem("shift_done")
        rstd_done = sem("rstd_done")
        xn_done = sem("xn_done")
        xt_turned = sem("xt_turned")
        xt_hi_done = sem("xt_hi_done")
        xt_lo_done = sem("xt_lo_done")
        proj_done = sem("proj_done")
        cos_done = sem("cos_done")
        cross_done = sem("cross_done")
        rot_done = sem("rot_done")
        v_hi_done = sem("v_hi_done")
        v_lo_done = sem("v_lo_done")
        qk_turned = sem("qk_turned")
        qk_hi_done = sem("qk_hi_done")
        qk_lo_done = sem("qk_lo_done")
        v_stored = [sem(f"v_stored{t}") for t in range(TILES)]
        qk_stored = [sem(f"qk_stored{t}") for t in range(TILES)]

        ORDER = [("X", 0), ("X", 1)]
        for t in range(TILES):
            ORDER.append(("J", t))
            if t + 2 < TILES:
                ORDER.append(("X", t + 2))
            if t:
                ORDER.append(("R", t - 1))
        ORDER.append(("R", TILES - 1))

        def value_columns(t, low):
            at = 64 if low else 0
            pairs = v[:, t, :].rearrange("p (j w) -> p j w", w=2 * P)
            return [pairs[:, :, at + e * (P + HEAD):at + e * (P + HEAD) + HEAD] for e in range(2)]

        def loop(eng, body):
            body(0, False)
            with eng.Fori(1, SEQS - 1) as s:
                body(s, False)
            body(SEQS - 1, True)

        def wait(eng, semaphore, count):
            if not (isinstance(count, int) and count <= 0):
                eng.wait_ge(semaphore, count)

        block = ctx.enter_context(nc.Block())

        @block.sync
        def _(sync):
            def tiles(dram, s):
                return dram[bass.ds(s * seq, seq), :].rearrange("(t p) n -> p t n", p=P)

            sync.dma_start(x[:], tiles(x_in, 0)).then_inc(x_loaded, 16)
            sync.dma_start(ident[:], ident_dram).then_inc(const_loaded, 16)
            at = 0
            for dram in (w_q, w_k, w_v):
                width = dram.shape[1]
                sync.dma_start(w[:, :, at:at + width], dram.rearrange("(k p) n -> p k n", p=P)).then_inc(w_loaded, 16)
                at += width
            for table, dram in ((cos, cos_dram), (sin, sin_dram)):
                sync.dma_start(table[:], dram.rearrange("(t p) n -> p t n", p=P)).then_inc(const_loaded, 16)

            def body(s, last):
                if not last:
                    sync.wait_ge(xn_done, (s + 1) * TILES)
                    sync.dma_start(x[:], tiles(x_in, s + 1)).then_inc(x_loaded, 16)
                for step, t in ORDER:
                    if step == "J":
                        sync.wait_ge(v_lo_done, 2 * (s * TILES + t + 1))
                        sync.dma_start(v_out[bass.ds(s, 1), :, t, :].rearrange("s p n -> p (s n)"),
                                       v[:, t, :].bitcast(FP32)).then_inc(v_stored[t], 16)
                    if step == "R":
                        sync.wait_ge(qk_lo_done, s * TILES + t + 1)
                        cols = slice(t * P, (t + 1) * P)
                        for dram, part in ((qk_hi_out, qk_hi), (qk_lo_out, qk_lo)):
                            sync.dma_start(dram[bass.ds(s, 1), :, :, cols].rearrange("s p c n -> (s p) c n"),
                                           part[:, :, cols].bitcast(FP32)).then_inc(qk_stored[t], 16)

            loop(sync, body)
            for t in range(TILES):
                sync.wait_ge(v_stored[t], SEQS * 16)
                sync.wait_ge(qk_stored[t], SEQS * 32)

        @block.gpsimd
        def _(pool):
            pool.memset(power[:], -0.5).then_inc(power_set, 1)
            pool.memset(eps[:], EPS).then_inc(power_set, 1)
            pool.memset(v[:].bitcast(FP32), 0.0).then_inc(v_cleared, 1)
            pool.wait_ge(power_set, 2)
            with pool.Fori(0, SEQS) as s:
                pool.wait_ge(stats_done, (s + 1) * TILES)
                pool.tensor_tensor(shifted[:], moments[:, :, 1], eps[:], ALU.add).then_inc(shift_done, 1)
                pool.wait_ge(shift_done, s + 1)
                pool.tensor_tensor(rstd[:], shifted[:], power[:], ALU.pow).then_inc(rstd_done, 1)

        @block.scalar
        def _(act):
            act.wait_ge(w_loaded, 48)
            for k in range(KC):
                act.activation(w_hi[:, k, :], w[:, k, :], ACT.Copy).then_inc(w_hi_done, 1)
            act.wait_ge(v_cleared, 1)

            def body(s, last):
                for step, t in ORDER:
                    tile = s * TILES + t
                    if step == "X":
                        act.wait_ge(xt_turned, tile + 1)
                        wait(act, proj_done, tile - 1 if t else tile)
                        act.activation(xt_hi[:, t % 2], xbank[:, t % 2, :].rearrange("p (k c) -> p k c", k=KC),
                                       ACT.Copy).then_inc(xt_hi_done, 1)
                    if step == "J":
                        act.wait_ge(proj_done, tile + 1)
                        wait(act, v_stored[t], s * 16)
                        values = proj[:, t % 2, QK:ALL].rearrange("p (j e d) -> p j e d", e=2, d=HEAD)
                        for e, out in enumerate(value_columns(t, False)):
                            act.activation(out, values[:, :, e, :], ACT.Copy).then_inc(v_hi_done, 1)
                    if step == "R":
                        act.wait_ge(qk_turned, tile + 1)
                        wait(act, qk_stored[t], s * 32)
                        act.activation(qk_hi[:, :, t * P:(t + 1) * P], qbank[:, 0:QK].rearrange("p (c n) -> p c n", n=P),
                                       ACT.Copy).then_inc(qk_hi_done, 1)

            loop(act, body)

        @block.vector
        def _(dve):
            def tile_stats(s):
                dve.wait_ge(x_loaded, (s + 1) * 16)
                for t in range(TILES):
                    dve.bn_stats(stats[:, t, :], x[:, t, :])
                dve.drain()
                for t in range(TILES):
                    dve.bn_aggr(moments[:, t, :], stats[:, t, :]).then_inc(stats_done, 1)

            tile_stats(0)
            for k in range(KC):
                dve.wait_ge(w_hi_done, k + 1)
                dve.tensor_tensor(w_lo[:, k, :], w[:, k, :], w_hi[:, k, :].bitcast(FP32),
                                  ALU.subtract).then_inc(w_lo_done, 1)
            dve.wait_ge(const_loaded, 48)

            def body(s, last):
                dve.wait_ge(rstd_done, s + 1)
                wait(dve, xt_turned, s * TILES)
                for t in range(TILES):
                    dve.tensor_scalar(xn[:, t, :], x[:, t, :], moments[:, t, 0:1], rstd[:, t:t + 1],
                                      ALU.subtract, ALU.mult).then_inc(xn_done, 1)
                for step, t in ORDER:
                    tile = s * TILES + t
                    if step == "X":
                        dve.wait_ge(xt_hi_done, tile + 1)
                        dve.tensor_tensor(xt_lo[:, t % 2], xbank[:, t % 2, :].rearrange("p (k c) -> p k c", k=KC),
                                          xt_hi[:, t % 2].bitcast(FP32), ALU.subtract).then_inc(xt_lo_done, 1)
                    if step == "J":
                        both = proj[:, t % 2, 0:QK]
                        dve.wait_ge(v_hi_done, 2 * tile + 2)
                        if t >= 2:
                            dve.wait_ge(qk_turned, tile - 1)
                        dve.tensor_tensor(rot[:, t % 2, :], both, cos[:, t, :], ALU.mult).then_inc(cos_done, 1)
                        wait(dve, rot_done, tile)
                        dve.tensor_tensor(cross[:, 0:QK:2], both[:, 1:QK:2], sin[:, t, 0:QK:2],
                                          ALU.mult).then_inc(cross_done, 1)
                        dve.tensor_tensor(cross[:, 1:QK:2], both[:, 0:QK:2], sin[:, t, 1:QK:2],
                                          ALU.mult).then_inc(cross_done, 1)
                        for e in range(2):
                            values = proj[:, t % 2, QK:ALL].rearrange("p (j e d) -> p j e d", e=2, d=HEAD)
                            dve.tensor_tensor(value_columns(t, True)[e], values[:, :, e, :],
                                              value_columns(t, False)[e].bitcast(FP32),
                                              ALU.subtract).then_inc(v_lo_done, 1)
                        dve.wait_ge(cos_done, tile + 1)
                        dve.wait_ge(cross_done, 2 * tile + 2)
                        dve.tensor_tensor(rot[:, t % 2, :], rot[:, t % 2, :], cross[:], ALU.add).then_inc(rot_done, 1)
                    if step == "R":
                        dve.wait_ge(qk_hi_done, tile + 1)
                        cols = slice(t * P, (t + 1) * P)
                        dve.tensor_tensor(qk_lo[:, :, cols], qbank[:, 0:QK].rearrange("p (c n) -> p c n", n=P),
                                          qk_hi[:, :, cols].bitcast(FP32), ALU.subtract).then_inc(qk_lo_done, 1)
                        if t == 0 and not last:
                            tile_stats(s + 1)

            loop(dve, body)

        @block.tensor
        def _(pe):
            pe.wait_ge(const_loaded, 48)
            pe.wait_ge(w_lo_done, KC)

            def body(s, last):
                for step, t in ORDER:
                    tile = s * TILES + t
                    if step == "X":
                        pe.wait_ge(xn_done, tile + 1)
                        wait(pe, xt_lo_done, tile - 1 if t else tile)
                        for k in range(KC):
                            last_one = nc.tensor.transpose(xbank[:, t % 2, k * P:(k + 1) * P],
                                                           xn[:, t, k * P:(k + 1) * P], ident[:])
                        last_one.then_inc(xt_turned, 1)
                    if step == "J":
                        pe.wait_ge(xt_lo_done, tile + 1)
                        wait(pe, v_lo_done, 2 * (tile - 1) if t else 2 * tile)
                        for at, width in ((0, N), (N, ALL - N)):
                            for k in range(KC):
                                for i, (xx, ww) in enumerate(((xt_hi, w_hi), (xt_hi, w_lo), (xt_lo, w_hi))):
                                    last_one = nc.tensor.matmul(proj[:, t % 2, at:at + width], xx[:, t % 2, k, :],
                                                                ww[:, k, at:at + width], start=k == 0 and i == 0,
                                                                stop=k == KC - 1 and i == 2)
                        last_one.then_inc(proj_done, 1)
                    if step == "R":
                        pe.wait_ge(rot_done, tile + 1)
                        wait(pe, qk_lo_done, tile)
                        for c in range(CH):
                            last_one = nc.tensor.transpose(qbank[:, c * P:(c + 1) * P],
                                                           rot[:, t % 2, c * P:(c + 1) * P], ident[:])
                        last_one.then_inc(qk_turned, 1)

            loop(pe, body)


def attention_phase(nc, ident_dram, qk_hi, qk_lo, v_in, w_o, x_in, x_out, seq):
    TOKENS, H = x_in.shape
    TILES = seq // P
    SEQS = TOKENS // seq
    CHUNKS = H // P
    HEADS = P // HEAD
    PAIRS = 2 * CHUNKS
    STEPS = 2 * TILES
    PLANES = P // HEAD
    TURN = 2
    TURNS = SEQS // TURN
    SLOTS = PAIRS * STEPS + CHUNKS + TILES
    LOADS = 6 * HEADS

    ctx = ExitStack()
    with ctx:
        def sb(name, shape, dtype=FP32):
            return ctx.enter_context(nc.sbuf_tensor(f"attn_{name}", shape, dtype))

        def ps(name, shape):
            return ctx.enter_context(nc.psum_tensor(f"attn_{name}", shape, FP32))

        def sem(name):
            return ctx.enter_context(nc.semaphore(f"attn_{name}"))

        qk = sb("qk", [P, TURN, CHUNKS + 1, HEADS, seq], FP32R)
        v = sb("v", [P, TURN, TILES, HEADS * P], FP32R)
        e = sb("e", [P, 2, TILES, 2, seq])
        p_hi = sb("p_hi", [P, 2, seq], FP32R)
        p_lo = sb("p_lo", [P, 2, seq], FP32R)
        w = sb("w", [P, CHUNKS, H])
        w_hi = sb("w_hi", [P, CHUNKS, H], FP32R)
        w_lo = sb("w_lo", [P, CHUNKS, H], FP32R)
        x = sb("x", [P, TILES, H])
        o = sb("o", [P, seq])
        o_low = sb("o_low", [P // 2, seq])
        o_hi = sb("o_hi", [P, CHUNKS, seq], FP32R)
        o_lo = sb("o_lo", [P, CHUNKS, seq], FP32R)
        neg_max = sb("neg_max", [P, 2, TILES, 2])
        sums = sb("sums", [P, 2, TILES, HEADS])
        inverse = sb("inverse", [P, TILES, HEADS])
        inverse_wide = sb("inverse_wide", [P, TILES, HEADS, HEAD])
        ones = sb("ones", [P, TILES, HEADS, HEAD])
        ident = sb("ident", [P, P])

        scores = ps("scores", [P, 2, 2, seq])
        shared = ps("shared", [P, 2, N])
        out_t = ps("out_t", [P, 2, seq])

        const_loaded = sem("const_loaded")
        qk_loaded = [sem("qk_loaded0"), sem("qk_loaded1")]
        v_loaded = [sem("v_loaded0"), sem("v_loaded1")]
        x_loaded = sem("x_loaded")
        x_stored = sem("x_stored")
        w_hi_done = sem("w_hi_done")
        w_lo_done = sem("w_lo_done")
        ones_set = sem("ones_set")
        scores_done = sem("scores_done")
        max_done = sem("max_done")
        exp_done = sem("exp_done")
        shared_written = sem("shared_written")
        shared_read = sem("shared_read")
        p_hi_done = sem("p_hi_done")
        pv_done = sem("pv_done")
        o_low_done = sem("o_low_done")
        o_added = sem("o_added")
        inverse_done = sem("inverse_done")
        wide_done = sem("wide_done")
        o_hi_done = sem("o_hi_done")
        o_lo_done = sem("o_lo_done")

        SCORES_AT = {0: 0, 1: 1, 3: 2, 5: 3}

        def order(first, last):
            found, slot = [], 0

            def add(step, pair, k=0):
                nonlocal slot
                uses = step in ("turn", "norm", "out")
                found.append((step, pair, k, slot if uses else None))
                slot += uses

            for pair in range(TURN * PAIRS):
                before = not (first and pair == 0)
                add("turn", pair, 0)
                if pair % 2:
                    add("inverse", pair)
                for s in range(STEPS):
                    if s == 2 and pair % 2 == 0 and before:
                        add("norm", pair)
                    if s + 1 < STEPS:
                        add("turn", pair, s + 1)
                    if s - 1 in SCORES_AT and not (last and pair == TURN * PAIRS - 1):
                        add("exp", pair, SCORES_AT[s - 1])
                    if s in SCORES_AT and not (last and pair == TURN * PAIRS - 1):
                        add("scores", pair, SCORES_AT[s])
                    add("value", pair, s)
                    if s == 1 and before:
                        add("join", pair)
                    if s == 2 and pair % 2 == 0 and before:
                        add("out_hi", pair)
                    if s == 3 and pair % 2 == 0 and before:
                        add("out_lo", pair)
                    if pair % PAIRS == 1 and s % 2 == 0 and not (first and pair == 1):
                        add("out", pair, s // 2)
            return found

        END = [("join", 0, 0, None), ("norm", 0, 0, 0), ("out_hi", 0, 0, None), ("out_lo", 0, 0, None)]
        END += [("out", 1, t, 1 + t) for t in range(TILES)]
        SKIPPED = 1 + TILES

        def slots_before(turn, first):
            return 0 if first else turn * (TURN * SLOTS) - SKIPPED

        def bank(first, slot):
            return slot % 2 if first else (TURN * SLOTS - SKIPPED + slot) % 2

        def loop(eng, body):
            body(0, order(True, TURNS == 1), True)
            if TURNS > 2:
                with eng.Fori(1, TURNS - 1) as turn:
                    body(turn, order(False, False), False)
            if TURNS > 1:
                body(TURNS - 1, order(False, True), False)
            body(TURNS, END, False)

        block = ctx.enter_context(nc.Block())

        @block.sync
        def _(sync):
            def load_qk(s, b):
                for planes, dram, part in ((0, qk_hi, None), (1, qk_lo, "q"), (1, qk_hi, "k"),
                                           (2, qk_hi, "q"), (2, qk_lo, "k"), (3, qk_lo, None)):
                    chunks = {None: slice(0, CHUNKS + 1), "q": slice(0, CHUNKS), "k": slice(CHUNKS, CHUNKS + 1)}[part]
                    rows = slice(planes * HEAD, (planes + 1) * HEAD)
                    for i in range(HEADS):
                        src = dram[bass.ds(s, 1), i * HEAD:(i + 1) * HEAD, chunks, :]
                        sync.dma_start(qk[rows, b, chunks, i, :].bitcast(FP32),
                                       src.rearrange("s p c n -> (s p) c n")).then_inc(qk_loaded[b], 16)

            def load_v(s, b):
                sync.dma_start(v[:, b].bitcast(FP32),
                               v_in[bass.ds(s, 1)].rearrange("s p t n -> (s p) t n")).then_inc(v_loaded[b], 16)

            def tiles(dram, s):
                return dram[bass.ds(s * seq, seq), :].rearrange("(t p) n -> p t n", p=P)

            sync.dma_start(ident[:], ident_dram).then_inc(const_loaded, 16)
            sync.dma_start(w[:], w_o.rearrange("(c p) n -> p c n", p=P)).then_inc(const_loaded, 16)
            for b in range(TURN):
                load_qk(b, b)
                load_v(b, b)

            def store(turn, half, first):
                steps = order(first, False)
                slot = [k for step, pair, _, k in steps if step == "out" and pair // PAIRS == half][-1]
                sync.wait_ge(shared_read, slots_before(turn, first) + slot + 1)
                sync.dma_start(tiles(x_out, turn * TURN + half - 1), x[:]).then_inc(x_stored, 16)
                sync.wait_ge(x_stored, (turn * TURN + half) * 16)

            def body(turn, first, last):
                for half in range(TURN):
                    s = turn * TURN + half
                    if not (first and half == 0):
                        store(turn, half, first)
                    sync.dma_start(x[:], tiles(x_in, s)).then_inc(x_loaded, 16)
                    if not last:
                        sync.wait_ge(scores_done, (s + 1) * (PAIRS * TILES))
                        load_qk(s + TURN, half)
                        sync.wait_ge(pv_done, (s + 1) * (PAIRS * STEPS))
                        load_v(s + TURN, half)

            body(0, True, TURNS == 1)
            if TURNS > 2:
                with sync.Fori(1, TURNS - 1) as turn:
                    body(turn, False, False)
            if TURNS > 1:
                body(TURNS - 1, False, True)
            sync.wait_ge(shared_read, slots_before(TURNS, False) + SKIPPED)
            sync.dma_start(tiles(x_out, SEQS - 1), x[:]).then_inc(x_stored, 16)
            sync.wait_ge(x_stored, SEQS * 16)

        @block.gpsimd
        def _(pool):
            pool.memset(ones[:], 1.0).then_inc(ones_set, 1)
            pool.wait_ge(ones_set, 1)
            with pool.Fori(0, SEQS * CHUNKS) as chunk:
                pool.wait_ge(inverse_done, chunk + 1)
                pool.tensor_tensor(inverse_wide[:], inverse[:].unsqueeze(3).broadcast_to((P, TILES, HEADS, HEAD)),
                                   ones[:], ALU.mult).then_inc(wide_done, 1)

        @block.scalar
        def _(act):
            def exponentials(n, nb, pair, t):
                act.wait_ge(max_done, n * TILES + t + 1)
                for i in range(2):
                    act.activation(e[:, nb, t, i, :], scores[:, t % 2, i, :], ACT.Exp,
                                   bias=neg_max[:, nb, t, i:i + 1],
                                   accum_out=sums[:, pair // 2 % 2, t, 2 * (pair % 2) + i:2 * (pair % 2) + i + 1]
                                   ).then_inc(exp_done, 1)

            act.wait_ge(const_loaded, 32)
            for c in range(CHUNKS):
                act.activation(w_hi[:, c, :], w[:, c, :], ACT.Copy).then_inc(w_hi_done, 1)
            for t in range(TILES):
                exponentials(0, 0, 0, t)

            def body(turn, steps, first):
                base = slots_before(turn, first)
                for step, pair, k, slot in steps:
                    n = turn * (TURN * PAIRS) + pair
                    if step == "turn":
                        act.wait_ge(shared_written, base + slot + 1)
                        if not (first and pair == 0 and k < 2):
                            act.wait_ge(pv_done, n * STEPS + k - 1)
                        act.activation(p_hi[:, k % 2, :], shared[:, bank(first, slot), :], ACT.Copy).then_inc(p_hi_done, 1)
                    if step == "exp":
                        exponentials(n + 1, (pair + 1) % 2, pair + 1, k)
                    if step == "join":
                        act.wait_ge(pv_done, n * STEPS)
                        if not (first and pair == 1):
                            act.wait_ge(o_added, n - 1)
                        act.activation(o_low[:], out_t[P // 2:P, (pair + 1) % 2, :], ACT.Copy).then_inc(o_low_done, 1)
                    if step == "norm":
                        norm_slot = slot
                    if step == "out_hi":
                        act.wait_ge(shared_read, base + norm_slot + 1)
                        act.activation(o_hi[:, (pair // 2 - 1) % CHUNKS, :], o[:], ACT.Copy).then_inc(o_hi_done, 1)

            loop(act, body)

        @block.vector
        def _(dve):
            def maxima(n, nb, t):
                dve.wait_ge(scores_done, n * TILES + t + 1)
                dve.tensor_reduce(neg_max[:, nb, t, :], scores[:, t % 2], AX.X, ALU.max,
                                  negate=True).then_inc(max_done, 1)

            for c in range(CHUNKS):
                dve.wait_ge(w_hi_done, c + 1)
                dve.tensor_tensor(w_lo[:, c, :], w[:, c, :], w_hi[:, c, :].bitcast(FP32),
                                  ALU.subtract).then_inc(w_lo_done, 1)
            for t in range(TILES):
                maxima(0, 0, t)

            def body(turn, steps, first):
                base = slots_before(turn, first)
                for step, pair, k, slot in steps:
                    n = turn * (TURN * PAIRS) + pair
                    chunks = turn * (TURN * CHUNKS) + pair // 2
                    if step == "turn":
                        dve.wait_ge(p_hi_done, n * STEPS + k + 1)
                        dve.tensor_tensor(p_lo[:, k % 2, :], shared[:, bank(first, slot), :],
                                          p_hi[:, k % 2, :].bitcast(FP32), ALU.subtract).then_inc(shared_read, 1)
                    if step == "scores":
                        maxima(n + 1, (pair + 1) % 2, k)
                    if step == "join":
                        dve.wait_ge(o_low_done, n)
                        rows = slice((pair + 1) % 2 * (P // 2), (pair + 1) % 2 * (P // 2) + P // 2)
                        dve.tensor_tensor(o[rows, :], out_t[0:P // 2, (pair + 1) % 2, :], o_low[:],
                                          ALU.add).then_inc(o_added, 1)
                    if step == "inverse":
                        dve.wait_ge(exp_done, (n + 1) * (2 * TILES))
                        if not (first and pair == 1):
                            dve.wait_ge(wide_done, chunks)
                        dve.reciprocal(inverse[:], sums[:, pair // 2 % 2]).then_inc(inverse_done, 1)
                    if step == "norm":
                        dve.wait_ge(shared_written, base + slot + 1)
                        dve.wait_ge(o_added, n)
                        dve.tensor_tensor(o[:], o[:], shared[:, bank(first, slot), :], ALU.mult).then_inc(shared_read, 1)
                        norm_slot = slot
                    if step == "out_lo":
                        dve.wait_ge(shared_read, base + norm_slot + 1)
                        dve.wait_ge(o_hi_done, chunks)
                        c = (pair // 2 - 1) % CHUNKS
                        dve.tensor_tensor(o_lo[:, c, :], o[:], o_hi[:, c, :].bitcast(FP32),
                                          ALU.subtract).then_inc(o_lo_done, 1)
                    if step == "out":
                        dve.wait_ge(shared_written, base + slot + 1)
                        if k == 0:
                            dve.wait_ge(x_loaded, (turn * TURN + pair // PAIRS) * 16)
                        dve.tensor_tensor(x[:, k, :], x[:, k, :], shared[:, bank(first, slot), :],
                                          ALU.add).then_inc(shared_read, 1)

            loop(dve, body)

        @block.tensor
        def _(pe):
            def score_products(turn, nb, pair, n, t, first):
                if pair % PAIRS == 0 and t == 0:
                    pe.wait_ge(qk_loaded[nb], (turn + 1) * (LOADS * 16))
                if not (first and t < 2):
                    pe.wait_ge(exp_done, (n * TILES + t - 1) * 2)
                c, pair_in = pair % PAIRS // 2, pair % 2
                for i in range(2):
                    head = 2 * pair_in + i
                    last_one = nc.tensor.matmul(scores[:, t % 2, i, :], qk[:, nb, c, head, t * P:(t + 1) * P],
                                                qk[:, nb, CHUNKS, head, :], start=True, stop=True)
                last_one.then_inc(scores_done, 1)

            pe.wait_ge(const_loaded, 32)
            for t in range(TILES):
                score_products(0, 0, 0, 0, t, True)

            def free(base, slot, first):
                if not (first and slot < 2):
                    pe.wait_ge(shared_read, base + slot - 1)

            def body(turn, steps, first):
                base = slots_before(turn, first)
                slot_of = {(pair, k): slot for step, pair, k, slot in steps if step == "turn"}
                for step, pair, k, slot in steps:
                    n = turn * (TURN * PAIRS) + pair
                    s_buf = pair // PAIRS
                    if step == "turn":
                        if k == 0:
                            pe.wait_ge(exp_done, (n + 1) * (2 * TILES))
                        free(base, slot, first)
                        i, c = k // TILES, k % TILES
                        for t in range(TILES):
                            last_one = nc.tensor.transpose(shared[:, bank(first, slot), t * P:(t + 1) * P],
                                                           e[:, pair % 2, t, i, c * P:(c + 1) * P], ident[:])
                        last_one.then_inc(shared_written, 1)
                    if step == "scores":
                        after = pair + 1
                        wraps = after == TURN * PAIRS
                        score_products(turn + 1 if wraps else turn, after // PAIRS % TURN, after, n + 1, k, False)
                    if step == "value":
                        if k == 0 and pair % PAIRS == 0:
                            pe.wait_ge(v_loaded[s_buf], (turn + 1) * 16)
                        if k == 0 and not (first and pair < 2):
                            pe.wait_ge(o_added, n - 1)
                        pe.wait_ge(shared_read, base + slot_of[pair, k] + 1)
                        i, c = k // TILES, k % TILES
                        at = (2 * (pair % 2) + i) * P
                        high = (out_t[:, pair % 2, :], v[:, s_buf, c, at:at + P], p_hi[:, k % 2, :])
                        low = (out_t[0:P // 2, pair % 2, :], v[:, s_buf, c, at:at + P // 2], p_lo[:, k % 2, :])
                        end = k == STEPS - 1
                        for j, (out, vv, pp) in enumerate((low, high) if end else (high, low)):
                            last_one = nc.tensor.matmul(out, vv, pp, start=k == 0 and j == 0, stop=end and j == 1)
                        last_one.then_inc(pv_done, 1)
                    if step == "norm":
                        pe.wait_ge(wide_done, turn * (TURN * CHUNKS) + pair // 2)
                        free(base, slot, first)
                        for t in range(TILES):
                            last_one = nc.tensor.transpose(shared[:, bank(first, slot), t * P:(t + 1) * P],
                                                           inverse_wide[:, t].rearrange("p h d -> p (h d)"), ident[:])
                        last_one.then_inc(shared_written, 1)
                    if step == "out":
                        if k == 0:
                            pe.wait_ge(w_lo_done, CHUNKS)
                            pe.wait_ge(o_lo_done, (turn * TURN + pair // PAIRS) * CHUNKS)
                        free(base, slot, first)
                        for c in range(CHUNKS):
                            for j, (oo, ww) in enumerate(((o_hi, w_hi), (o_hi, w_lo), (o_lo, w_hi))):
                                last_one = nc.tensor.matmul(shared[:, bank(first, slot), :], oo[:, c, k * P:(k + 1) * P],
                                                            ww[:, c, :], start=c == 0 and j == 0,
                                                            stop=c == CHUNKS - 1 and j == 2)
                        last_one.then_inc(shared_written, 1)

            loop(pe, body)




def macaron_layer(nc, ident, cos, sin, x, w_q, w_k, w_v, w_o, w_gate, w_up, w_down, out):
    seqs, seq, hidden = x.shape
    heads = w_k.shape[1] // HEAD
    chunks = w_q.shape[1] // P

    def scratch(name, shape):
        return nc.dram_tensor(name, shape, FP32, kind="Internal").ap()

    tokens_in, tokens_out = (a.rearrange("b s n -> (b s) n") for a in (x, out))
    after_ffn = scratch("after_ffn", (seqs * seq, hidden))
    after_attention = scratch("after_attention", (seqs * seq, hidden))
    qk_hi = scratch("qk_hi", (seqs, P, chunks + 1, seq))
    qk_lo = scratch("qk_lo", (seqs, P, chunks + 1, seq))
    values = scratch("values", (seqs, P, seq // P, heads * P))

    ffn_phase(nc, ident, tokens_in, after_ffn, w_gate, w_up, w_down, "ffn1")
    qkv_phase(nc, ident, cos, sin, after_ffn, w_q, w_k, w_v, qk_hi, qk_lo, values, seq)
    attention_phase(nc, ident, qk_hi, qk_lo, values, w_o, after_ffn, after_attention, seq)
    ffn_phase(nc, ident, after_attention, tokens_out, w_gate, w_up, w_down, "ffn2")


def rotation_tables(seq, query_columns, key_columns):
    half = HEAD // 2
    freqs = (1.0 / np.float32(10000.0) ** (np.arange(half, dtype=np.float32) / np.float32(half))).astype(np.float32)
    angles = np.arange(seq, dtype=np.float32)[:, None] * freqs[None, :]
    cos = np.repeat(np.cos(angles), 2, axis=1)
    sin = np.repeat(np.sin(angles), 2, axis=1)
    sin[:, 0::2] *= -1.0
    scale = np.ones((1, query_columns + key_columns), np.float32)
    scale[:, :query_columns] = HEAD ** -0.5
    copies = (query_columns + key_columns) // HEAD
    return [(np.tile(a, (1, copies)) * scale).astype(np.float32) for a in (cos, sin)]


_INS = ["L0_attn_x", "L0_attn_W_q", "L0_attn_W_k", "L0_attn_W_v", "L0_attn_W_o",
        "L0_ffn_w_gate", "L0_ffn_w_up", "L0_ffn_w_down"]


def kernel(**inputs):
    import concourse.bacc as _bacc
    from concourse.bass_utils import run_bass_kernel_spmd as _run

    nc = _bacc.Bacc("TRN2", target_bir_lowering=False, num_devices=1)
    seq = inputs["L0_attn_x"].shape[1]
    cos, sin = rotation_tables(seq, inputs["L0_attn_W_q"].shape[1], inputs["L0_attn_W_k"].shape[1])
    arrays = {"identity": np.eye(P, dtype=np.float32), "cosines": cos, "sines": sin}
    arrays.update({name: np.ascontiguousarray(inputs[name]) for name in _INS})
    args = [nc.dram_tensor(n, a.shape, mybir.dt.from_np(a.dtype), kind="ExternalInput").ap() for n, a in arrays.items()]
    out = nc.dram_tensor("out", inputs["L0_attn_x"].shape, FP32, kind="ExternalOutput").ap()
    macaron_layer(nc, *args, out)
    return _run(nc, [arrays], core_ids=[0]).results[0]["out"]
```

```python
from contextlib import ExitStack

import numpy as np

import concourse.bass as bass
from concourse import mybir

FP32 = mybir.dt.float32
FP32R = mybir.dt.float32r
BF16 = mybir.dt.bfloat16
ALU = mybir.AluOpType
ACT = mybir.ActivationFunctionType
AX = mybir.AxisListType

P = 128
N = 512
EPS = 1e-5
HEAD = 32


def ffn_phase(nc, ident_dram, x_in, x_out, w_gate, w_up, w_down, tag):
    TOKENS, H = x_in.shape
    I = w_gate.shape[1]
    KC = H // P
    SUB = N // P
    GROUP = 2 * N
    GROUPS = TOKENS // GROUP
    BLOCKS = I // N
    R = 4
    UNITS = 2 * BLOCKS
    QUARTERS = 6
    STEPS = 10

    ctx = ExitStack()
    with ctx:
        def sb(name, shape, dtype=FP32):
            return ctx.enter_context(nc.sbuf_tensor(f"{tag}_{name}", shape, dtype))

        def sem(name):
            return ctx.enter_context(nc.semaphore(f"{tag}_{name}"))

        w_hi = sb("w_hi", [P, 2, 3, R * N], FP32R)
        w_lo = sb("w_lo", [P, 2, 3, R * N], FP32R)
        stage = sb("stage", [P, 2, 2, N])
        xt_hi = sb("xt_hi", [P, KC, GROUP], FP32R)
        xt_lo = sb("xt_lo", [P, KC, GROUP], FP32R)
        xn = sb("xn", [P, SUB, H])
        acc = sb("acc", [P, 2, SUB, H])
        h = sb("h", [P, R, N])
        hs_hi = sb("hs_hi", [P, R, N], FP32R)
        hs_lo = sb("hs_lo", [P, R, N], FP32R)
        mag = sb("mag", [P, R, N])
        top = sb("top", [P, 2, N])
        first = sb("first", [P, 2, N], BF16)
        both = sb("both", [P, 2, N], BF16)
        split = sb("split", [P, 2, N], BF16)
        keep = sb("keep", [P, R, N], BF16)
        ident = sb("ident", [P, P])
        stats = sb("stats", [P, SUB, 6])
        moments = sb("moments", [P, SUB, 2])
        shifted = sb("shifted", [P, SUB])
        rstd = sb("rstd", [P, SUB])
        power = sb("power", [P, SUB])
        eps = sb("eps", [P, SUB])

        gu = ctx.enter_context(nc.psum_tensor(f"{tag}_gu", [P, 2, 2, N], FP32))
        y = ctx.enter_context(nc.psum_tensor(f"{tag}_y", [P, SUB, H], FP32))

        ident_loaded = sem("ident_loaded")
        stage_loaded = [sem("stage_loaded0"), sem("stage_loaded1")]
        xn_loaded = sem("xn_loaded")
        acc_loaded = [sem("acc_loaded0"), sem("acc_loaded1")]
        acc_stored = [sem("acc_stored0"), sem("acc_stored1")]
        w_hi_done = sem("w_hi_done")
        w_lo_done = sem("w_lo_done")
        stats_done = sem("stats_done")
        power_set = sem("power_set")
        shift_done = sem("shift_done")
        rstd_done = sem("rstd_done")
        xn_done = sem("xn_done")
        xt_turned = sem("xt_turned")
        xt_hi_done = sem("xt_hi_done")
        xt_lo_done = sem("xt_lo_done")
        gu_done = sem("gu_done")
        silu_done = sem("silu_done")
        h_done = sem("h_done")
        mag_done = sem("mag_done")
        mask_step = sem("mask_step")
        masked = sem("masked")
        hs_hi_done = sem("hs_hi_done")
        hs_lo_done = sem("hs_lo_done")
        down_done = sem("down_done")
        y_added = sem("y_added")

        even, odd = mag[:, 0:R:2, :], mag[:, 1:R:2, :]
        def pieces(u):
            b, half = u // 2, u % 2
            start = b * QUARTERS + (0 if half == 0 else 2)
            gaps = (0, 1) if half == 0 else (0, 1, 2, 2)
            return [(g, start + k) for k, g in enumerate(gaps)]

        def piece_views(q, b):
            kind, part = q // 2, q % 2
            w = [w_hi[:, b, kind, :], w_lo[:, b, kind, :]]
            if kind < 2:
                dst = [v.rearrange("p (k r c) -> p k r c", k=KC, r=R)[:, 2 * part:2 * part + 2] for v in w]
                return dst, lambda s: s.rearrange("p k (c r) -> p k r c", r=R)
            dst = [v.rearrange("p (r n) -> p r n", r=R)[:, 2 * part:2 * part + 2, :] for v in w]
            return dst, lambda s: s

        def last_units(last):
            return UNITS - 2 if last else UNITS

        def loop(eng, body):
            body(0, True, False)
            if GROUPS > 2:
                with eng.Fori(1, GROUPS - 1) as g:
                    body(g, False, False)
            body(GROUPS - 1, False, True)

        block = ctx.enter_context(nc.Block())

        @block.sync
        def _(sync):
            def load_piece(g, n):
                block_of, q = n // QUARTERS % BLOCKS, n % QUARTERS
                kind, part = q // 2, q % 2
                count = g * (BLOCKS * QUARTERS) + n
                if n >= 2:
                    sync.wait_ge(w_lo_done, count - 1)
                if kind < 2:
                    src = (w_gate, w_up)[kind].rearrange("(k p) i -> p k i", p=P)
                    src = src[:, 2 * part:2 * part + 2, block_of * N:(block_of + 1) * N]
                else:
                    src = w_down.rearrange("(b p r) n -> b p r n", p=P, r=R)[block_of, :, 2 * part:2 * part + 2, :]
                sync.dma_start(stage[:, n % 2], src).then_inc(stage_loaded[n % 2], 16)

            def rows(g, half):
                return bass.ds(g * GROUP + half * N, N)

            def tiles(dram, g, half):
                return dram[rows(g, half), :].rearrange("(t p) n -> p t n", p=P)

            def store(g, half):
                sync.wait_ge(y_added, (g * UNITS + UNITS - 1 + half) * SUB)
                sync.dma_start(tiles(x_out, g, half), acc[:, half]).then_inc(acc_stored[half], 16)

            def reload(g, half):
                sync.wait_ge(acc_stored[half], g * 16)
                sync.dma_start(acc[:, half], tiles(x_in, g, half)).then_inc(acc_loaded[half], 16)

            sync.dma_start(xn[:], tiles(x_in, 0, 0)).then_inc(xn_loaded, 16)
            sync.dma_start(ident[:], ident_dram).then_inc(ident_loaded, 16)
            for n in range(4):
                load_piece(0, n)
            sync.wait_ge(xt_turned, SUB)
            sync.dma_start(xn[:], tiles(x_in, 0, 1)).then_inc(xn_loaded, 16)
            for n in range(4, QUARTERS):
                load_piece(0, n)
            for half in range(2):
                sync.dma_start(acc[:, half], tiles(x_in, 0, half)).then_inc(acc_loaded[half], 16)
            for n in range(2):
                load_piece(0, QUARTERS + n)

            def body(g, first, last):
                end = QUARTERS * (BLOCKS - 1) if last else QUARTERS * BLOCKS + 2
                for u in range(UNITS):
                    for _, c in pieces(u):
                        if c + 2 < end:
                            load_piece(g, QUARTERS + c + 2)
                    if u == 0 and not first:
                        store(g - 1, 1)
                        reload(g, 1)
                    if u == UNITS - 3 and not last:
                        sync.wait_ge(xt_turned, g * 2 * SUB + 2 * SUB)
                        sync.dma_start(xn[:], tiles(x_in, g + 1, 0)).then_inc(xn_loaded, 16)
                if not last:
                    sync.wait_ge(xt_turned, g * 2 * SUB + 3 * SUB)
                    sync.dma_start(xn[:], tiles(x_in, g + 1, 1)).then_inc(xn_loaded, 16)
                store(g, 0)
                if not last:
                    reload(g + 1, 0)

            loop(sync, body)
            store(GROUPS - 1, 1)
            for half in range(2):
                sync.wait_ge(acc_stored[half], GROUPS * 16)

        @block.gpsimd
        def _(pool):
            pool.memset(power[:], -0.5).then_inc(power_set, 1)
            pool.memset(eps[:], EPS).then_inc(power_set, 1)
            pool.wait_ge(power_set, 2)
            with pool.Fori(0, 2 * GROUPS) as i:
                pool.wait_ge(stats_done, (i + 1) * SUB)
                pool.tensor_tensor(shifted[:], moments[:, :, 1], eps[:], ALU.add).then_inc(shift_done, 1)
                pool.wait_ge(shift_done, i + 1)
                pool.tensor_tensor(rstd[:], shifted[:], power[:], ALU.pow).then_inc(rstd_done, 1)

        @block.scalar
        def _(act):
            def split_piece(g, n):
                q, b = n % QUARTERS, n // QUARTERS % 2
                count = g * (BLOCKS * QUARTERS) + n
                act.wait_ge(stage_loaded[n % 2], (g * (BLOCKS * QUARTERS // 2) + n // 2 + 1) * 16)
                dst, view = piece_views(q, b)
                act.activation(dst[0], view(stage[:, n % 2]), ACT.Copy).then_inc(w_hi_done, 1)

            def tile_hi(count, half, t):
                act.wait_ge(xt_turned, count + 1)
                at = half * N + t * P
                act.activation(xt_hi[:, :, at:at + P], gu[:, t // 2, t % 2, :].rearrange("p (k c) -> p k c", k=KC),
                               ACT.Copy).then_inc(xt_hi_done, 1)

            for n in range(2):
                split_piece(0, n)
            for t in range(SUB):
                tile_hi(t, 0, t)
            for n in range(2, 4):
                split_piece(0, n)

            def body(g, first, last):
                for u in range(UNITS):
                    unit = g * UNITS + u
                    splits = pieces(u) if u < last_units(last) else []
                    for r in range(R):
                        act.wait_ge(gu_done, unit * R + r + 1)
                        if not (first and u == 0):
                            act.wait_ge(hs_lo_done, unit * R - R + r + 1)
                        act.activation(h[:, r, :], gu[:, r % 2, 0, :], ACT.Silu).then_inc(silu_done, 1)
                        if first and u == 0 and r == 0:
                            for n in range(4, QUARTERS):
                                split_piece(0, n)
                        for gap, c in splits:
                            if gap == r:
                                if not (first and u < 2):
                                    act.wait_ge(gu_done if c % QUARTERS < 4 else down_done, (g * UNITS + u - u % 2) * R)
                                split_piece(g, QUARTERS + c)
                        if r >= 2:
                            pair = r - 2
                            act.wait_ge(h_done, unit * R + 2 * pair + 2)
                            act.activation(mag[:, 2 * pair:2 * pair + 2, :], h[:, 2 * pair:2 * pair + 2, :],
                                           ACT.Abs).then_inc(mag_done, 1)
                    if u == 0:
                        for t in range(SUB):
                            tile_hi(g * 2 * SUB + SUB + t, 1, t)
                    if u == UNITS - 1 and not last:
                        for t in range(SUB):
                            tile_hi(g * 2 * SUB + 2 * SUB + t, 0, t)
                    for r in range(R):
                        act.wait_ge(masked, unit * R + r + 1)
                        if not (first and u == 0):
                            act.wait_ge(down_done, unit * R - R + r + 1)
                        act.activation(hs_hi[:, r, :], h[:, r, :], ACT.Copy).then_inc(hs_hi_done, 1)

            loop(act, body)

        @block.vector
        def _(dve):
            def split_piece(g, n):
                q, b = n % QUARTERS, n // QUARTERS % 2
                dst, view = piece_views(q, b)
                dve.wait_ge(w_hi_done, g * (BLOCKS * QUARTERS) + n + 1)
                dve.tensor_tensor(dst[1], view(stage[:, n % 2]), dst[0].bitcast(FP32),
                                  ALU.subtract).then_inc(w_lo_done, 1)

            def tile_lo(count, half, t):
                dve.wait_ge(xt_hi_done, count + 1)
                at = half * N + t * P
                dve.tensor_tensor(xt_lo[:, :, at:at + P], gu[:, t // 2, t % 2, :].rearrange("p (k c) -> p k c", k=KC),
                                  xt_hi[:, :, at:at + P].bitcast(FP32), ALU.subtract).then_inc(xt_lo_done, 1)

            def tile_stats(k):
                dve.wait_ge(xn_loaded, (k + 1) * 16)
                for t in range(SUB):
                    dve.bn_stats(stats[:, t, :], xn[:, t, :])
                dve.drain()
                for t in range(SUB):
                    dve.bn_aggr(moments[:, t, :], stats[:, t, :]).then_inc(stats_done, 1)

            def tile_norm(k):
                dve.wait_ge(rstd_done, k + 1)
                for t in range(SUB):
                    dve.tensor_scalar(xn[:, t, :], xn[:, t, :], moments[:, t, 0:1], rstd[:, t:t + 1],
                                      ALU.subtract, ALU.mult).then_inc(xn_done, 1)

            def add_block(g, u):
                half = u % 2
                dve.wait_ge(down_done, (g * UNITS + u + 1) * R)
                if u < 2:
                    dve.wait_ge(acc_loaded[half], (g + 1) * 16)
                else:
                    dve.wait_ge(y_added, (g * UNITS + u - 1) * SUB)
                for t in range(SUB):
                    dve.scalar_tensor_tensor(acc[:, half, t, :], y[:, t, :], 0.5, acc[:, half, t, :],
                                             ALU.mult, ALU.add).then_inc(y_added, 1)

            def choose(unit):
                step = unit * STEPS
                dve.wait_ge(mag_done, unit * 2 + 2)
                dve.tensor_tensor(first[:], even, odd, ALU.is_ge).then_inc(mask_step, 1)
                dve.tensor_tensor(top[:], even, odd, ALU.max).then_inc(mask_step, 1)
                dve.wait_ge(mask_step, step + 2)
                dve.tensor_tensor(even, even, odd, ALU.min).then_inc(mask_step, 1)
                dve.wait_ge(mask_step, step + 3)
                dve.tensor_tensor(both[:, 0, :], mag[:, 0, :], top[:, 1, :], ALU.is_ge).then_inc(mask_step, 1)
                dve.tensor_tensor(both[:, 1, :], mag[:, 2, :], top[:, 0, :], ALU.is_gt).then_inc(mask_step, 1)
                dve.wait_ge(mask_step, step + 5)
                dve.tensor_scalar(split[:, 0, :], both[:, 1, :], -1.0, 1.0, ALU.mult, ALU.add).then_inc(mask_step, 1)
                dve.tensor_scalar(split[:, 1, :], both[:, 0, :], -1.0, 1.0, ALU.mult, ALU.add).then_inc(mask_step, 1)
                dve.wait_ge(mask_step, step + 7)
                dve.tensor_tensor(keep[:, 0:R:2, :], first[:], split[:], ALU.mult).then_inc(mask_step, 1)
                dve.wait_ge(mask_step, step + 8)
                dve.tensor_tensor(keep[:, 1:R:2, :], split[:], keep[:, 0:R:2, :], ALU.subtract).then_inc(mask_step, 1)
                dve.wait_ge(mask_step, step + 9)
                pairs = keep[:].rearrange("p (a e) n -> p a e n", e=2)
                dve.tensor_tensor(pairs, pairs, both[:].unsqueeze(2).broadcast_to((P, 2, 2, N)),
                                  ALU.max).then_inc(mask_step, 1)

            def apply(unit):
                dve.wait_ge(mask_step, unit * STEPS + STEPS)
                for r in range(R):
                    dve.tensor_tensor(h[:, r, :], h[:, r, :], keep[:, r, :], ALU.mult).then_inc(masked, 1)
                for r in range(R):
                    dve.wait_ge(hs_hi_done, unit * R + r + 1)
                    dve.tensor_tensor(hs_lo[:, r, :], h[:, r, :], hs_hi[:, r, :].bitcast(FP32),
                                      ALU.subtract).then_inc(hs_lo_done, 1)

            tile_stats(0)
            for n in range(2):
                split_piece(0, n)
            tile_norm(0)
            for t in range(SUB):
                tile_lo(t, 0, t)
            for n in range(2, 4):
                split_piece(0, n)

            def body(g, first, last):
                for u in range(UNITS):
                    unit = g * UNITS + u
                    splits = pieces(u) if u < last_units(last) else []
                    for r in range(R):
                        dve.wait_ge(silu_done, unit * R + r + 1)
                        dve.tensor_tensor(h[:, r, :], h[:, r, :], gu[:, r % 2, 1, :], ALU.mult).then_inc(h_done, 1)
                        if first and u == 0 and r == 0:
                            for n in range(4, QUARTERS):
                                split_piece(0, n)
                        for gap, c in splits:
                            if gap == r:
                                split_piece(g, QUARTERS + c)
                        if u == 0 and r == 0:
                            tile_stats(2 * g + 1)
                        if u == 0 and r == 1:
                            tile_norm(2 * g + 1)
                        if u == UNITS - 2 and r == 2 and not last:
                            tile_stats(2 * g + 2)
                        if u == UNITS - 1 and r == 1 and not last:
                            tile_norm(2 * g + 2)
                    choose(unit)
                    if u == 0:
                        for t in range(SUB):
                            tile_lo(g * 2 * SUB + SUB + t, 1, t)
                    if u == UNITS - 1 and not last:
                        for t in range(SUB):
                            tile_lo(g * 2 * SUB + 2 * SUB + t, 0, t)
                    apply(unit)
                    if u:
                        add_block(g, u - 1)
                    elif not first:
                        add_block(g - 1, UNITS - 1)

            loop(dve, body)
            add_block(GROUPS - 1, UNITS - 1)

        @block.tensor
        def _(pe):
            def gate_up(g, u, r, first):
                unit, b = g * UNITS + u, u // 2 % 2
                half = u % 2
                if r == 0:
                    if u < 2:
                        pe.wait_ge(xt_lo_done, g * 2 * SUB + (u + 1) * SUB)
                    if half == 0:
                        pe.wait_ge(w_lo_done, g * (BLOCKS * QUARTERS) + u // 2 * QUARTERS + 4)
                if not (first and u == 0 and r < 2):
                    pe.wait_ge(h_done, unit * R + r - 1)
                for kind in range(2):
                    whi = w_hi[:, b, kind, :].rearrange("p (k r c) -> p k r c", k=KC, r=R)
                    wlo = w_lo[:, b, kind, :].rearrange("p (k r c) -> p k r c", k=KC, r=R)
                    for k in range(KC):
                        xh = xt_hi[:, k, half * N:(half + 1) * N]
                        xl = xt_lo[:, k, half * N:(half + 1) * N]
                        for i, (w, x) in enumerate(((whi, xh), (whi, xl), (wlo, xh))):
                            last = nc.tensor.matmul(gu[:, r % 2, kind, :], w[:, k, r, :], x,
                                                    start=k == 0 and i == 0, stop=k == KC - 1 and i == 2)
                last.then_inc(gu_done, 1)

            def down(g, u, turned=None):
                unit, b = g * UNITS + u, u // 2 % 2
                if not (isinstance(unit, int) and unit == 0):
                    pe.wait_ge(y_added, unit * SUB)
                if u % 2 == 0:
                    pe.wait_ge(w_lo_done, g * (BLOCKS * QUARTERS) + u // 2 * QUARTERS + 6)
                for r in range(R):
                    if r == R // 2 and turned is not None:
                        turn_half(turned, unit + 1)
                    pe.wait_ge(hs_lo_done, unit * R + r + 1)
                    wh = w_hi[:, b, 2, r * N:(r + 1) * N]
                    wl = w_lo[:, b, 2, r * N:(r + 1) * N]
                    for t in range(SUB):
                        at = slice(t * P, (t + 1) * P)
                        for i, (x, w) in enumerate(((hs_hi, wh), (hs_hi, wl), (hs_lo, wh))):
                            last = nc.tensor.matmul(y[:, t, :], x[:, r, at], w, start=r == 0 and i == 0,
                                                    stop=r == R - 1 and i == 2)
                    last.then_inc(down_done, 1)

            def turn(count, t):
                pe.wait_ge(xn_done, count + 1)
                for k in range(KC):
                    last = nc.tensor.transpose(gu[:, t // 2, t % 2, k * P:(k + 1) * P], xn[:, t, k * P:(k + 1) * P],
                                               ident[:])
                last.then_inc(xt_turned, 1)

            def turn_half(count, unit):
                pe.wait_ge(h_done, (unit + 1) * R)
                for t in range(SUB):
                    turn(count + t, t)

            pe.wait_ge(ident_loaded, 16)
            for t in range(SUB):
                turn(t, t)

            def body(g, first, last):
                for u in range(UNITS):
                    for r in range(R):
                        gate_up(g, u, r, first)
                    if u == 0:
                        second = g * 2 * SUB + SUB
                        if first:
                            turn_half(second, g * UNITS)
                        else:
                            down(g - 1, UNITS - 1, second)
                    elif u == UNITS - 1 and not last:
                        down(g, u - 1, g * 2 * SUB + 2 * SUB)
                    else:
                        down(g, u - 1)

            loop(pe, body)
            down(GROUPS - 1, UNITS - 1)


def qkv_phase(nc, ident_dram, cos_dram, sin_dram, x_in, w_q, w_k, w_v, qk_hi_out, qk_lo_out, v_out, seq):
    TOKENS, H = x_in.shape
    KC = H // P
    TILES = seq // P
    SEQS = TOKENS // seq
    DQ, DK = w_q.shape[1], w_k.shape[1]
    QK = DQ + DK
    ALL = QK + DK
    CH = QK // P
    KVH = DK // HEAD
    VW = 3 * (P // 2)

    ctx = ExitStack()
    with ctx:
        def sb(name, shape, dtype=FP32):
            return ctx.enter_context(nc.sbuf_tensor(f"qkv_{name}", shape, dtype))

        def ps(name, shape):
            return ctx.enter_context(nc.psum_tensor(f"qkv_{name}", shape, FP32))

        def sem(name):
            return ctx.enter_context(nc.semaphore(f"qkv_{name}"))

        w = sb("w", [P, KC, ALL])
        w_hi = sb("w_hi", [P, KC, ALL], FP32R)
        w_lo = sb("w_lo", [P, KC, ALL], FP32R)
        cos = sb("cos", [P, TILES, QK])
        sin = sb("sin", [P, TILES, QK])
        ident = sb("ident", [P, P])
        x = sb("x", [P, TILES, H])
        xn = sb("xn", [P, TILES, H])
        xt_hi = sb("xt_hi", [P, 2, KC, P], FP32R)
        xt_lo = sb("xt_lo", [P, 2, KC, P], FP32R)
        rot = sb("rot", [P, 2, QK])
        cross = sb("cross", [P, QK])
        qk_hi = sb("qk_hi", [P, CH, seq], FP32R)
        qk_lo = sb("qk_lo", [P, CH, seq], FP32R)
        v = sb("v", [P, TILES, KVH * VW], FP32R)
        stats = sb("stats", [P, TILES, 6])
        moments = sb("moments", [P, TILES, 2])
        shifted = sb("shifted", [P, TILES])
        rstd = sb("rstd", [P, TILES])
        power = sb("power", [P, TILES])
        eps = sb("eps", [P, TILES])

        xbank = ps("xbank", [P, 2, KC * P])
        proj = ps("proj", [P, 2, 2 * N])
        qbank = ps("qbank", [P, 2 * N])

        const_loaded = sem("const_loaded")
        w_loaded = sem("w_loaded")
        x_loaded = sem("x_loaded")
        w_hi_done = sem("w_hi_done")
        w_lo_done = sem("w_lo_done")
        v_cleared = sem("v_cleared")
        stats_done = sem("stats_done")
        power_set = sem("power_set")
        shift_done = sem("shift_done")
        rstd_done = sem("rstd_done")
        xn_done = sem("xn_done")
        xt_turned = sem("xt_turned")
        xt_hi_done = sem("xt_hi_done")
        xt_lo_done = sem("xt_lo_done")
        proj_done = sem("proj_done")
        cos_done = sem("cos_done")
        cross_done = sem("cross_done")
        rot_done = sem("rot_done")
        v_hi_done = sem("v_hi_done")
        v_lo_done = sem("v_lo_done")
        qk_turned = sem("qk_turned")
        qk_hi_done = sem("qk_hi_done")
        qk_lo_done = sem("qk_lo_done")
        v_stored = [sem(f"v_stored{t}") for t in range(TILES)]
        qk_stored = [sem(f"qk_stored{t}") for t in range(TILES)]

        ORDER = [("X", 0), ("X", 1)]
        for t in range(TILES):
            ORDER.append(("J", t))
            if t + 2 < TILES:
                ORDER.append(("X", t + 2))
            if t:
                ORDER.append(("R", t - 1))
        ORDER.append(("R", TILES - 1))

        def value_columns(t, part):
            pairs = v[:, t, :].rearrange("p (j w) -> p j w", w=2 * VW)
            at = part * (P // 2)
            return [pairs[:, :, at + e * (VW + HEAD):at + e * (VW + HEAD) + HEAD] for e in range(2)]

        def loop(eng, body):
            body(0, False)
            with eng.Fori(1, SEQS - 1) as s:
                body(s, False)
            body(SEQS - 1, True)

        def wait(eng, semaphore, count):
            if not (isinstance(count, int) and count <= 0):
                eng.wait_ge(semaphore, count)

        block = ctx.enter_context(nc.Block())

        @block.sync
        def _(sync):
            def tiles(dram, s):
                return dram[bass.ds(s * seq, seq), :].rearrange("(t p) n -> p t n", p=P)

            sync.dma_start(x[:], tiles(x_in, 0)).then_inc(x_loaded, 16)
            sync.dma_start(ident[:], ident_dram).then_inc(const_loaded, 16)
            at = 0
            for dram in (w_q, w_k, w_v):
                width = dram.shape[1]
                sync.dma_start(w[:, :, at:at + width], dram.rearrange("(k p) n -> p k n", p=P)).then_inc(w_loaded, 16)
                at += width
            for table, dram in ((cos, cos_dram), (sin, sin_dram)):
                sync.dma_start(table[:], dram.rearrange("(t p) n -> p t n", p=P)).then_inc(const_loaded, 16)

            def body(s, last):
                if not last:
                    sync.wait_ge(xn_done, (s + 1) * TILES)
                    sync.dma_start(x[:], tiles(x_in, s + 1)).then_inc(x_loaded, 16)
                for step, t in ORDER:
                    if step == "J":
                        sync.wait_ge(v_lo_done, 2 * (s * TILES + t + 1))
                        sync.dma_start(v_out[bass.ds(s, 1), :, t, :].rearrange("s p n -> p (s n)"),
                                       v[:, t, :].bitcast(FP32)).then_inc(v_stored[t], 16)
                    if step == "R":
                        sync.wait_ge(qk_lo_done, s * TILES + t + 1)
                        cols = slice(t * P, (t + 1) * P)
                        for dram, part in ((qk_hi_out, qk_hi), (qk_lo_out, qk_lo)):
                            sync.dma_start(dram[bass.ds(s, 1), :, :, cols].rearrange("s p c n -> (s p) c n"),
                                           part[:, :, cols].bitcast(FP32)).then_inc(qk_stored[t], 16)

            loop(sync, body)
            for t in range(TILES):
                sync.wait_ge(v_stored[t], SEQS * 16)
                sync.wait_ge(qk_stored[t], SEQS * 32)

        @block.gpsimd
        def _(pool):
            pool.memset(power[:], -0.5).then_inc(power_set, 1)
            pool.memset(eps[:], EPS).then_inc(power_set, 1)
            pool.memset(v[:].bitcast(FP32), 0.0).then_inc(v_cleared, 1)
            pool.wait_ge(v_cleared, 1)
            for t in range(TILES):
                for ones in value_columns(t, 1):
                    pool.memset(ones.bitcast(FP32), 1.0).then_inc(v_cleared, 1)
            pool.wait_ge(power_set, 2)
            with pool.Fori(0, SEQS) as s:
                pool.wait_ge(stats_done, (s + 1) * TILES)
                pool.tensor_tensor(shifted[:], moments[:, :, 1], eps[:], ALU.add).then_inc(shift_done, 1)
                pool.wait_ge(shift_done, s + 1)
                pool.tensor_tensor(rstd[:], shifted[:], power[:], ALU.pow).then_inc(rstd_done, 1)

        @block.scalar
        def _(act):
            act.wait_ge(w_loaded, 48)
            for k in range(KC):
                act.activation(w_hi[:, k, :], w[:, k, :], ACT.Copy).then_inc(w_hi_done, 1)
            act.wait_ge(v_cleared, 1 + 2 * TILES)

            def body(s, last):
                for step, t in ORDER:
                    tile = s * TILES + t
                    if step == "X":
                        act.wait_ge(xt_turned, tile + 1)
                        wait(act, proj_done, tile - 1 if t else tile)
                        act.activation(xt_hi[:, t % 2], xbank[:, t % 2, :].rearrange("p (k c) -> p k c", k=KC),
                                       ACT.Copy).then_inc(xt_hi_done, 1)
                    if step == "J":
                        act.wait_ge(proj_done, tile + 1)
                        wait(act, v_stored[t], s * 16)
                        values = proj[:, t % 2, QK:ALL].rearrange("p (j e d) -> p j e d", e=2, d=HEAD)
                        for e, out in enumerate(value_columns(t, 0)):
                            act.activation(out, values[:, :, e, :], ACT.Copy).then_inc(v_hi_done, 1)
                    if step == "R":
                        act.wait_ge(qk_turned, tile + 1)
                        wait(act, qk_stored[t], s * 32)
                        act.activation(qk_hi[:, :, t * P:(t + 1) * P], qbank[:, 0:QK].rearrange("p (c n) -> p c n", n=P),
                                       ACT.Copy).then_inc(qk_hi_done, 1)

            loop(act, body)

        @block.vector
        def _(dve):
            def tile_stats(s):
                dve.wait_ge(x_loaded, (s + 1) * 16)
                for t in range(TILES):
                    dve.bn_stats(stats[:, t, :], x[:, t, :])
                dve.drain()
                for t in range(TILES):
                    dve.bn_aggr(moments[:, t, :], stats[:, t, :]).then_inc(stats_done, 1)

            tile_stats(0)
            for k in range(KC):
                dve.wait_ge(w_hi_done, k + 1)
                dve.tensor_tensor(w_lo[:, k, :], w[:, k, :], w_hi[:, k, :].bitcast(FP32),
                                  ALU.subtract).then_inc(w_lo_done, 1)
            dve.wait_ge(const_loaded, 48)

            def body(s, last):
                dve.wait_ge(rstd_done, s + 1)
                wait(dve, xt_turned, s * TILES)
                for t in range(TILES):
                    dve.tensor_scalar(xn[:, t, :], x[:, t, :], moments[:, t, 0:1], rstd[:, t:t + 1],
                                      ALU.subtract, ALU.mult).then_inc(xn_done, 1)
                for step, t in ORDER:
                    tile = s * TILES + t
                    if step == "X":
                        dve.wait_ge(xt_hi_done, tile + 1)
                        dve.tensor_tensor(xt_lo[:, t % 2], xbank[:, t % 2, :].rearrange("p (k c) -> p k c", k=KC),
                                          xt_hi[:, t % 2].bitcast(FP32), ALU.subtract).then_inc(xt_lo_done, 1)
                    if step == "J":
                        both = proj[:, t % 2, 0:QK]
                        dve.wait_ge(v_hi_done, 2 * tile + 2)
                        if t >= 2:
                            dve.wait_ge(qk_turned, tile - 1)
                        dve.tensor_tensor(rot[:, t % 2, :], both, cos[:, t, :], ALU.mult).then_inc(cos_done, 1)
                        wait(dve, rot_done, tile)
                        dve.tensor_tensor(cross[:, 0:QK:2], both[:, 1:QK:2], sin[:, t, 0:QK:2],
                                          ALU.mult).then_inc(cross_done, 1)
                        dve.tensor_tensor(cross[:, 1:QK:2], both[:, 0:QK:2], sin[:, t, 1:QK:2],
                                          ALU.mult).then_inc(cross_done, 1)
                        for e in range(2):
                            values = proj[:, t % 2, QK:ALL].rearrange("p (j e d) -> p j e d", e=2, d=HEAD)
                            dve.tensor_tensor(value_columns(t, 2)[e], values[:, :, e, :],
                                              value_columns(t, 0)[e].bitcast(FP32),
                                              ALU.subtract).then_inc(v_lo_done, 1)
                        dve.wait_ge(cos_done, tile + 1)
                        dve.wait_ge(cross_done, 2 * tile + 2)
                        dve.tensor_tensor(rot[:, t % 2, :], rot[:, t % 2, :], cross[:], ALU.add).then_inc(rot_done, 1)
                    if step == "R":
                        dve.wait_ge(qk_hi_done, tile + 1)
                        cols = slice(t * P, (t + 1) * P)
                        dve.tensor_tensor(qk_lo[:, :, cols], qbank[:, 0:QK].rearrange("p (c n) -> p c n", n=P),
                                          qk_hi[:, :, cols].bitcast(FP32), ALU.subtract).then_inc(qk_lo_done, 1)
                        if t == 0 and not last:
                            tile_stats(s + 1)

            loop(dve, body)

        @block.tensor
        def _(pe):
            pe.wait_ge(const_loaded, 48)
            pe.wait_ge(w_lo_done, KC)

            def body(s, last):
                for step, t in ORDER:
                    tile = s * TILES + t
                    if step == "X":
                        pe.wait_ge(xn_done, tile + 1)
                        wait(pe, xt_lo_done, tile - 1 if t else tile)
                        for k in range(KC):
                            last_one = nc.tensor.transpose(xbank[:, t % 2, k * P:(k + 1) * P],
                                                           xn[:, t, k * P:(k + 1) * P], ident[:])
                        last_one.then_inc(xt_turned, 1)
                    if step == "J":
                        pe.wait_ge(xt_lo_done, tile + 1)
                        wait(pe, v_lo_done, 2 * (tile - 1) if t else 2 * tile)
                        for at, width in ((0, N), (N, ALL - N)):
                            for k in range(KC):
                                for i, (xx, ww) in enumerate(((xt_hi, w_hi), (xt_hi, w_lo), (xt_lo, w_hi))):
                                    last_one = nc.tensor.matmul(proj[:, t % 2, at:at + width], xx[:, t % 2, k, :],
                                                                ww[:, k, at:at + width], start=k == 0 and i == 0,
                                                                stop=k == KC - 1 and i == 2)
                        last_one.then_inc(proj_done, 1)
                    if step == "R":
                        pe.wait_ge(rot_done, tile + 1)
                        wait(pe, qk_lo_done, tile)
                        for c in range(CH):
                            last_one = nc.tensor.transpose(qbank[:, c * P:(c + 1) * P],
                                                           rot[:, t % 2, c * P:(c + 1) * P], ident[:])
                        last_one.then_inc(qk_turned, 1)

            loop(pe, body)


def attention_phase(nc, ident_dram, qk_hi, qk_lo, v_in, w_o, x_in, x_out, seq):
    TOKENS, H = x_in.shape
    TILES = seq // P
    SEQS = TOKENS // seq
    CHUNKS = H // P
    HEADS = P // HEAD
    PLANES = 3
    AT_MAX = PLANES * HEAD
    HALVES = TILES // 2
    UNITS = HEADS * HALVES
    TURN = 2
    TURNS = SEQS // TURN
    TURN_CHUNKS = TURN * CHUNKS
    TURN_UNITS = TURN_CHUNKS * UNITS
    RING = 4
    VW = 3 * (P // 2)
    LOADS = 5 * HEADS

    ctx = ExitStack()
    with ctx:
        def sb(name, shape, dtype=FP32):
            return ctx.enter_context(nc.sbuf_tensor(f"attn_{name}", shape, dtype))

        def ps(name, shape):
            return ctx.enter_context(nc.psum_tensor(f"attn_{name}", shape, FP32))

        def sem(name):
            return ctx.enter_context(nc.semaphore(f"attn_{name}"))

        qk = sb("qk", [P, TURN, CHUNKS + 1, HEADS, seq], FP32R)
        v = sb("v", [P, TURN, TILES, HEADS * VW], FP32R)
        e = sb("e", [P, RING, 2, seq])
        p_hi = sb("p_hi", [P, RING, 2, seq], FP32R)
        p_lo = sb("p_lo", [P, RING, 2, seq], FP32R)
        w_hi = sb("w_hi", [P, CHUNKS, H], FP32R)
        w_lo = sb("w_lo", [P, CHUNKS, H], FP32R)
        x = sb("x", [P, TILES, H])
        o = sb("o", [P, seq])
        o_raw = sb("o_raw", [P, seq])
        sums = sb("sums", [P, seq])
        columns = sb("columns", [P, seq // HEAD, HEAD])
        inverse = sb("inverse", [P, seq // HEAD])
        o_hi = sb("o_hi", [P, CHUNKS, seq], FP32R)
        o_lo = sb("o_lo", [P, CHUNKS, seq], FP32R)
        neg_max = sb("neg_max", [P, 2, TILES, HEADS])
        max_parts = sb("max_parts", [P, TILES, 2, HEADS], FP32R)
        max_rows = sb("max_rows", [2 * HEADS, seq], FP32R)
        ident = sb("ident", [P, P])

        ring = ps("ring", [P, 2, seq])
        scores = ps("scores", [P, 2, 2, seq])
        out_t = ps("out_t", [P, 2, seq])

        ident_loaded = sem("ident_loaded")
        w_loaded = sem("w_loaded")
        qk_loaded = [sem("qk_loaded0"), sem("qk_loaded1")]
        v_loaded = [sem("v_loaded0"), sem("v_loaded1")]
        rows_loaded = sem("rows_loaded")
        x_loaded = sem("x_loaded")
        x_stored = sem("x_stored")
        ones_set = sem("ones_set")
        w_hi_done = sem("w_hi_done")
        w_lo_done = sem("w_lo_done")
        ring_written = sem("ring_written")
        ring_read = sem("ring_read")
        max_hi_done = sem("max_hi_done")
        max_lo_done = sem("max_lo_done")
        scores_done = sem("scores_done")
        exp_done = sem("exp_done")
        hi_by_act = sem("hi_by_act")
        hi_by_dve = sem("hi_by_dve")
        lo_by_pool = sem("lo_by_pool")
        lo_by_dve = sem("lo_by_dve")
        pv_done = sem("pv_done")
        joined = sem("joined")
        invert_step = sem("invert_step")
        o_done = sem("o_done")
        o_hi_done = sem("o_hi_done")
        o_lo_done = sem("o_lo_done")

        DVE_HI, DVE_LO = 1, 3

        def hi_count(turn, unit):
            if unit % 4 == DVE_HI:
                return True, turn * (TURN_UNITS // 4) + unit // 4 + 1
            before = unit // 4 * 3 + unit % 4 + (unit % 4 < DVE_HI)
            return False, turn * (TURN_UNITS // 4 * 3) + before

        def lo_count(turn, unit):
            if unit % 4 == DVE_LO:
                return True, turn * (TURN_UNITS // 4) + unit // 4 + 1
            return False, turn * (TURN_UNITS // 4 * 3) + unit // 4 * 3 + unit % 4 + 1

        def wait(eng, semaphore, count):
            if not (isinstance(count, int) and count <= 0):
                eng.wait_ge(semaphore, count)

        def wait_lo(eng, turn, unit):
            by_dve, count = lo_count(turn, unit)
            wait(eng, lo_by_dve if by_dve else lo_by_pool, count)

        def order(first, last):
            found, slot = [], 0

            def add(step, index, k=0, uses=False):
                nonlocal slot
                found.append((step, index, k, slot))
                slot += uses

            for j in range(TURN_UNITS):
                g, u = divmod(j, UNITS)
                more = not (last and g >= TURN_CHUNKS - 2)
                before = not (first and g == 0)
                if not (last and j + 4 >= TURN_UNITS):
                    add("scores", j + 4)
                if not (last and j + 3 >= TURN_UNITS):
                    add("exp", j + 3)
                if u == 0 and not (last and g == TURN_CHUNKS - 1):
                    add("max_split", g + 1)
                if more:
                    add("max", g + 2, 2 * u, True)
                add("value", j, 0)
                if u == UNITS // 2 or (u == 0 and before):
                    add("join", j // (UNITS // 2) - 1)
                if more:
                    add("max", g + 2, 2 * u + 1, True)
                add("value", j, 1)
                if not (last and j + 3 >= TURN_UNITS):
                    add("high", j + 3)
                if not (last and j + 2 >= TURN_UNITS):
                    add("low", j + 2)
                if u == 1 and before:
                    add("invert", g - 1)
                if u == 1 and not (last and g == TURN_CHUNKS - 1):
                    add("max_turn", g + 1, 0, True)
                if u == 2 and before:
                    add("o_split", g - 1)
                if g % CHUNKS == 0 and before and u >= UNITS - TILES:
                    add("out", g // CHUNKS, u - (UNITS - TILES), True)
                if first and g == 1 and u < CHUNKS:
                    add("w_split", u)
            return found

        START = [("max", 0, k, k) for k in range(HEADS * TILES)]
        START += [("max_split", 0, 0, len(START)), ("max_turn", 0, 0, len(START))]
        START += [("max", 1, k, len(START) - 1 + k) for k in range(HEADS * TILES)]
        START += [("scores", 0, 0, 0), ("exp", 0, 0, 0), ("high", 0, 0, 0), ("low", 0, 0, 0),
                  ("scores", 1, 0, 0), ("exp", 1, 0, 0), ("high", 1, 0, 0), ("low", 1, 0, 0),
                  ("scores", 2, 0, 0), ("exp", 2, 0, 0), ("high", 2, 0, 0), ("scores", 3, 0, 0)]
        END = [("join", -1, 0, 0), ("invert", -1, 0, 0), ("o_split", -1, 0, 0)] + [("out", 0, t, t) for t in range(TILES)]
        START_SLOTS = 2 * HEADS * TILES + 1
        TURN_SLOTS = TURN_CHUNKS * (HEADS * TILES + 1) + TURN * TILES

        def slots_before(turn, kind):
            if kind == "start":
                return 0
            if kind == "first":
                return START_SLOTS
            base = turn * TURN_SLOTS + START_SLOTS - TILES
            return base - (2 * HEADS * TILES + 1) if kind == "end" else base

        def parity(kind):
            return slots_before(0 if kind in ("start", "first") else TURNS if kind == "end" else 1, kind) % 2

        def loop(eng, body):
            body(0, START, "start")
            body(0, order(True, False), "first")
            if TURNS > 2:
                with eng.Fori(1, TURNS - 1) as turn:
                    body(turn, order(False, False), "middle")
            body(TURNS - 1, order(False, True), "last")
            body(TURNS, END, "end")

        block = ctx.enter_context(nc.Block())

        @block.sync
        def _(sync):
            def load_qk(s, b):
                for plane, dram, part in ((0, qk_hi, None), (1, qk_lo, "q"), (1, qk_hi, "k"),
                                          (2, qk_hi, "q"), (2, qk_lo, "k")):
                    chunks = {None: slice(0, CHUNKS + 1), "q": slice(0, CHUNKS), "k": slice(CHUNKS, CHUNKS + 1)}[part]
                    rows = slice(plane * HEAD, (plane + 1) * HEAD)
                    for i in range(HEADS):
                        src = dram[bass.ds(s, 1), i * HEAD:(i + 1) * HEAD, chunks, :]
                        sync.dma_start(qk[rows, b, chunks, i, :].bitcast(FP32),
                                       src.rearrange("s p c n -> (s p) c n")).then_inc(qk_loaded[b], 16)

            def load_v(s, b):
                sync.dma_start(v[:, b].bitcast(FP32),
                               v_in[bass.ds(s, 1)].rearrange("s p t n -> (s p) t n")).then_inc(v_loaded[b], 16)

            def tiles(dram, s):
                return dram[bass.ds(s * seq, seq), :].rearrange("(t p) n -> p t n", p=P)

            sync.dma_start(ident[:], ident_dram).then_inc(ident_loaded, 16)
            load_qk(0, 0)
            load_v(0, 0)
            sync.dma_start(x[:], w_o.rearrange("(c p) n -> p c n", p=P)).then_inc(w_loaded, 16)

            def body(turn, steps, kind):
                base = slots_before(turn, kind)
                for step, index, k, slot in steps:
                    if step == "max_turn":
                        sync.wait_ge(ring_read, base + slot + 1)
                        nb, c = index // CHUNKS % TURN, index % CHUNKS
                        for part in range(2):
                            at = AT_MAX + part
                            sync.dma_start(qk[at:at + 1, nb, c, :, :].bitcast(FP32),
                                           max_rows[part * HEADS:(part + 1) * HEADS, :].bitcast(FP32)
                                           ).then_inc(rows_loaded, 16)
                        if kind == "start":
                            load_qk(1, 1)
                            load_v(1, 1)
                        elif index % CHUNKS == 1:
                            half = index // CHUNKS
                            s = turn * TURN + half
                            if (kind, half) not in (("first", 0), ("last", 1)):
                                sync.wait_ge(pv_done, s * (CHUNKS * UNITS))
                                load_qk(s + 1, (half + 1) % TURN)
                                load_v(s + 1, (half + 1) % TURN)
                    if step == "w_split" and index == CHUNKS - 1:
                        sync.wait_ge(w_lo_done, CHUNKS)
                        sync.dma_start(x[:], tiles(x_in, 0)).then_inc(x_loaded, 16)
                    if step == "out" and k == TILES - 1:
                        sync.wait_ge(ring_read, base + slot + 1)
                        s = turn * TURN + index
                        sync.dma_start(tiles(x_out, s - 1), x[:]).then_inc(x_stored, 16)
                        sync.wait_ge(x_stored, s * 16)
                        if kind != "end":
                            sync.dma_start(x[:], tiles(x_in, s)).then_inc(x_loaded, 16)

            loop(sync, body)

        @block.gpsimd
        def _(pool):
            for b in range(TURN):
                pool.memset(qk[AT_MAX:AT_MAX + 2, b, CHUNKS, :, :].bitcast(FP32), 1.0).then_inc(ones_set, 1)

            def body(turn, steps, kind):
                for step, unit, _, _ in steps:
                    if step == "low" and unit % 4 != DVE_LO:
                        by_dve, count = hi_count(turn, unit)
                        pool.wait_ge(hi_by_dve if by_dve else hi_by_act, count)
                        pool.tensor_tensor(p_lo[:, unit % RING], e[:, unit % RING], p_hi[:, unit % RING].bitcast(FP32),
                                           ALU.subtract).then_inc(lo_by_pool, 1)

            loop(pool, body)

        @block.scalar
        def _(act):
            def body(turn, steps, kind):
                base = slots_before(turn, kind)
                for step, index, k, slot in steps:
                    unit = turn * TURN_UNITS + index
                    if step == "exp":
                        act.wait_ge(scores_done, unit + 1)
                        wait_lo(act, turn, index - RING)
                        act.activation(e[:, index % RING], scores[:, index % 2], ACT.Exp).then_inc(exp_done, 1)
                    if step == "high" and index % 4 != DVE_HI:
                        act.wait_ge(exp_done, unit + 1)
                        wait(act, pv_done, unit - RING + 1)
                        act.activation(p_hi[:, index % RING], e[:, index % RING], ACT.Copy).then_inc(hi_by_act, 1)
                    if step == "join":
                        pair = turn * (TURN_UNITS // 4) + index
                        act.wait_ge(pv_done, pair * 4 + 4)
                        if index % 2 == 0:
                            wait(act, o_done, turn * TURN_CHUNKS + index // 2)
                        rows = slice(index % 2 * (P // 2), (index % 2 + 1) * (P // 2))
                        for to, at in ((o_raw, 0), (sums, P // 2)):
                            act.activation(to[rows, :], out_t[at:at + P // 2, index % 2, :],
                                           ACT.Copy).then_inc(joined, 1)
                    if step == "max_split":
                        act.wait_ge(ring_read, base + slot)
                        act.activation(max_parts[:, :, 0, :], neg_max[:, index % 2], ACT.Copy).then_inc(max_hi_done, 1)
                    if step == "o_split":
                        chunk = turn * TURN_CHUNKS + index
                        act.wait_ge(o_done, chunk + 1)
                        if index % CHUNKS == 0:
                            act.wait_ge(ring_read, base + slot)
                        act.activation(o_hi[:, index % CHUNKS, :], o[:], ACT.Copy).then_inc(o_hi_done, 1)
                    if step == "w_split":
                        act.wait_ge(w_loaded, 16)
                        act.activation(w_hi[:, index, :], x[:, index, :], ACT.Copy).then_inc(w_hi_done, 1)

            loop(act, body)

        @block.vector
        def _(dve):
            def body(turn, steps, kind):
                base = slots_before(turn, kind)
                for step, index, k, slot in steps:
                    unit = turn * TURN_UNITS + index
                    bank = (parity(kind) + slot) % 2
                    if step == "max":
                        i, t = k // TILES, k % TILES
                        dve.wait_ge(ring_written, base + slot + 1)
                        dve.tensor_reduce(neg_max[:, index % 2, t, i:i + 1], ring[:, bank, :], AX.X, ALU.max,
                                          negate=True).then_inc(ring_read, 1)
                    if step == "max_split":
                        chunk = turn * TURN_CHUNKS + index
                        dve.wait_ge(max_hi_done, chunk + 1)
                        dve.tensor_tensor(max_parts[:, :, 1, :], neg_max[:, index % 2],
                                          max_parts[:, :, 0, :].bitcast(FP32), ALU.subtract).then_inc(max_lo_done, 1)
                    if step == "max_turn":
                        chunk = turn * TURN_CHUNKS + index
                        dve.wait_ge(ring_written, base + slot + 1)
                        wait(dve, rows_loaded, chunk * 32)
                        dve.tensor_copy(max_rows[:], ring[0:2 * HEADS, bank, :]).then_inc(ring_read, 1)
                    if step == "high" and index % 4 == DVE_HI:
                        dve.wait_ge(exp_done, unit + 1)
                        wait(dve, pv_done, unit - RING + 1)
                        dve.tensor_copy(p_hi[:, index % RING], e[:, index % RING]).then_inc(hi_by_dve, 1)
                    if step == "low" and index % 4 == DVE_LO:
                        dve.wait_ge(hi_by_act, hi_count(turn, index)[1])
                        dve.tensor_tensor(p_lo[:, index % RING], e[:, index % RING], p_hi[:, index % RING].bitcast(FP32),
                                          ALU.subtract).then_inc(lo_by_dve, 1)
                    if step == "invert":
                        chunk = turn * TURN_CHUNKS + index
                        dve.wait_ge(joined, chunk * 4 + 4)
                        dve.transpose(columns[:].rearrange("p b c -> p (b c)"), sums[:]).then_inc(invert_step, 1)
                        dve.wait_ge(invert_step, chunk * 3 + 1)
                        dve.reciprocal(inverse[:], columns[:, :, 0]).then_inc(invert_step, 1)
                        dve.wait_ge(invert_step, chunk * 3 + 2)
                        dve.transpose(sums[:].rearrange("p (b c) -> p b c", c=HEAD),
                                      inverse[:].unsqueeze(2).broadcast_to((P, seq // HEAD, HEAD))
                                      ).then_inc(invert_step, 1)
                    if step == "o_split":
                        chunk = turn * TURN_CHUNKS + index
                        dve.wait_ge(invert_step, chunk * 3 + 3)
                        wait(dve, o_lo_done, chunk)
                        dve.tensor_tensor(o[:], o_raw[:], sums[:], ALU.mult).then_inc(o_done, 1)
                        dve.wait_ge(o_hi_done, chunk + 1)
                        c = index % CHUNKS
                        dve.tensor_tensor(o_lo[:, c, :], o[:], o_hi[:, c, :].bitcast(FP32),
                                          ALU.subtract).then_inc(o_lo_done, 1)
                    if step == "out":
                        dve.wait_ge(ring_written, base + slot + 1)
                        if k == 0:
                            dve.wait_ge(x_loaded, (turn * TURN + index) * 16)
                        dve.tensor_tensor(x[:, k, :], x[:, k, :], ring[:, bank, :], ALU.add).then_inc(ring_read, 1)
                    if step == "w_split":
                        dve.wait_ge(w_hi_done, index + 1)
                        dve.tensor_tensor(w_lo[:, index, :], x[:, index, :], w_hi[:, index, :].bitcast(FP32),
                                          ALU.subtract).then_inc(w_lo_done, 1)

            loop(dve, body)

        @block.tensor
        def _(pe):
            pe.wait_ge(ones_set, TURN)

            def body(turn, steps, kind):
                base = slots_before(turn, kind)
                for step, index, k, slot in steps:
                    unit = turn * TURN_UNITS + index
                    bank = (parity(kind) + slot) % 2

                    def free():
                        if not (kind == "start" and slot < 2):
                            pe.wait_ge(ring_read, base + slot - 1)

                    if step == "max":
                        nb, c, i, t = index // CHUNKS % TURN, index % CHUNKS, k // TILES, k % TILES
                        if c == 0 and k == 0:
                            turns = turn + index // TURN_CHUNKS + 1
                            pe.wait_ge(qk_loaded[nb], turns * (LOADS * 16))
                        free()
                        nc.tensor.matmul(ring[:, bank, :], qk[0:AT_MAX, nb, c, i, t * P:(t + 1) * P],
                                         qk[0:AT_MAX, nb, CHUNKS, i, :], start=True, stop=True).then_inc(ring_written, 1)
                    if step == "max_turn":
                        if kind == "start":
                            pe.wait_ge(ident_loaded, 16)
                        pe.wait_ge(max_lo_done, turn * TURN_CHUNKS + index + 1)
                        free()
                        for t in range(TILES):
                            last_one = nc.tensor.transpose(ring[0:2 * HEADS, bank, t * P:(t + 1) * P],
                                                           max_parts[:, t].bitcast(FP32).rearrange("p a h -> p (a h)"),
                                                           ident[:])
                        last_one.then_inc(ring_written, 1)
                    if step == "scores":
                        g = index // UNITS
                        nb, c = g // CHUNKS % TURN, g % CHUNKS
                        i, half = index % UNITS // HALVES, index % HALVES
                        if index % UNITS == 0:
                            pe.wait_ge(rows_loaded, (turn * TURN_CHUNKS + g + 1) * 32)
                        wait(pe, exp_done, unit - 1)
                        for kc in range(2):
                            at = (half * 2 + kc) * P
                            last_one = nc.tensor.matmul(scores[:, index % 2, kc, :],
                                                        qk[0:AT_MAX + 2, nb, CHUNKS, i, at:at + P],
                                                        qk[0:AT_MAX + 2, nb, c, i, :], start=True, stop=True)
                        last_one.then_inc(scores_done, 1)
                    if step == "value":
                        g = index // UNITS
                        nb, i, half = g // CHUNKS, index % UNITS // HALVES, index % HALVES
                        pair = index // 4
                        if k == 0:
                            if index % (UNITS * CHUNKS) == 0:
                                pe.wait_ge(v_loaded[nb], (turn + 1) * 16)
                            if index % 4 == 0:
                                wait(pe, joined, (turn * (TURN_UNITS // 4) + pair - 1) * 2)
                            wait_lo(pe, turn, index)
                        at = i * VW
                        values = v[:, nb, half * 2 + k, at:at + VW]
                        ph, pl = p_hi[:, index % RING, k, :], p_lo[:, index % RING, k, :]
                        begins, ends = index % 4 == 0 and k == 0, index % 4 == 3 and k == 1
                        nc.tensor.matmul(out_t[:, pair % 2, :], values[:, 0:P], ph, start=begins, stop=False)
                        nc.tensor.matmul(out_t[0:P // 2, pair % 2, :], values[:, P:VW], ph, start=False, stop=False)
                        last_one = nc.tensor.matmul(out_t[:, pair % 2, :], values[:, 0:P], pl, start=False, stop=ends)
                        if k == 1:
                            last_one.then_inc(pv_done, 1)
                    if step == "out":
                        if k == 0:
                            pe.wait_ge(w_lo_done, CHUNKS)
                            pe.wait_ge(o_lo_done, (turn * TURN + index) * CHUNKS)
                        free()
                        for c in range(CHUNKS):
                            for j, (oo, ww) in enumerate(((o_hi, w_hi), (o_hi, w_lo), (o_lo, w_hi))):
                                last_one = nc.tensor.matmul(ring[:, bank, :], oo[:, c, k * P:(k + 1) * P],
                                                            ww[:, c, :], start=c == 0 and j == 0,
                                                            stop=c == CHUNKS - 1 and j == 2)
                        last_one.then_inc(ring_written, 1)

            loop(pe, body)




def macaron_layer(nc, ident, cos, sin, x, w_q, w_k, w_v, w_o, w_gate, w_up, w_down, out):
    seqs, seq, hidden = x.shape
    heads = w_k.shape[1] // HEAD
    chunks = w_q.shape[1] // P

    def scratch(name, shape):
        return nc.dram_tensor(name, shape, FP32, kind="Internal").ap()

    tokens_in, tokens_out = (a.rearrange("b s n -> (b s) n") for a in (x, out))
    after_ffn = scratch("after_ffn", (seqs * seq, hidden))
    after_attention = scratch("after_attention", (seqs * seq, hidden))
    qk_hi = scratch("qk_hi", (seqs, P, chunks + 1, seq))
    qk_lo = scratch("qk_lo", (seqs, P, chunks + 1, seq))
    values = scratch("values", (seqs, P, seq // P, heads * 3 * (P // 2)))

    ffn_phase(nc, ident, tokens_in, after_ffn, w_gate, w_up, w_down, "ffn1")
    qkv_phase(nc, ident, cos, sin, after_ffn, w_q, w_k, w_v, qk_hi, qk_lo, values, seq)
    attention_phase(nc, ident, qk_hi, qk_lo, values, w_o, after_ffn, after_attention, seq)
    ffn_phase(nc, ident, after_attention, tokens_out, w_gate, w_up, w_down, "ffn2")


def rotation_tables(seq, query_columns, key_columns):
    half = HEAD // 2
    freqs = (1.0 / np.float32(10000.0) ** (np.arange(half, dtype=np.float32) / np.float32(half))).astype(np.float32)
    angles = np.arange(seq, dtype=np.float32)[:, None] * freqs[None, :]
    cos = np.repeat(np.cos(angles), 2, axis=1)
    sin = np.repeat(np.sin(angles), 2, axis=1)
    sin[:, 0::2] *= -1.0
    scale = np.ones((1, query_columns + key_columns), np.float32)
    scale[:, :query_columns] = HEAD ** -0.5
    copies = (query_columns + key_columns) // HEAD
    return [(np.tile(a, (1, copies)) * scale).astype(np.float32) for a in (cos, sin)]


_INS = ["L0_attn_x", "L0_attn_W_q", "L0_attn_W_k", "L0_attn_W_v", "L0_attn_W_o",
        "L0_ffn_w_gate", "L0_ffn_w_up", "L0_ffn_w_down"]


def kernel(**inputs):
    import concourse.bacc as _bacc
    from concourse.bass_utils import run_bass_kernel_spmd as _run

    nc = _bacc.Bacc("TRN2", target_bir_lowering=False, num_devices=1)
    seq = inputs["L0_attn_x"].shape[1]
    cos, sin = rotation_tables(seq, inputs["L0_attn_W_q"].shape[1], inputs["L0_attn_W_k"].shape[1])
    arrays = {"identity": np.eye(P, dtype=np.float32), "cosines": cos, "sines": sin}
    arrays.update({name: np.ascontiguousarray(inputs[name]) for name in _INS})
    args = [nc.dram_tensor(n, a.shape, mybir.dt.from_np(a.dtype), kind="ExternalInput").ap() for n, a in arrays.items()]
    out = nc.dram_tensor("out", inputs["L0_attn_x"].shape, FP32, kind="ExternalOutput").ap()
    macaron_layer(nc, *args, out)
    return _run(nc, [arrays], core_ids=[0]).results[0]["out"]
```

```python
from contextlib import ExitStack

import numpy as np

import concourse.bass as bass
from concourse import mybir

FP32 = mybir.dt.float32
FP32R = mybir.dt.float32r
BF16 = mybir.dt.bfloat16
ALU = mybir.AluOpType
ACT = mybir.ActivationFunctionType
AX = mybir.AxisListType

P = 128
N = 512
EPS = 1e-5
HEAD = 32


def ffn_phase(nc, ident_dram, x_in, x_out, w_gate, w_up, w_down, tag):
    TOKENS, H = x_in.shape
    I = w_gate.shape[1]
    KC = H // P
    SUB = N // P
    GROUP = 2 * N
    GROUPS = TOKENS // GROUP
    BLOCKS = I // N
    R = 4
    UNITS = 2 * BLOCKS
    QUARTERS = 6
    STEPS = 10

    ctx = ExitStack()
    with ctx:
        def sb(name, shape, dtype=FP32):
            return ctx.enter_context(nc.sbuf_tensor(f"{tag}_{name}", shape, dtype))

        def sem(name):
            return ctx.enter_context(nc.semaphore(f"{tag}_{name}"))

        w_hi = sb("w_hi", [P, 2, 3, R * N], FP32R)
        w_lo = sb("w_lo", [P, 2, 3, R * N], FP32R)
        stage = sb("stage", [P, 2, 2, N])
        xt_hi = sb("xt_hi", [P, KC, GROUP], FP32R)
        xt_lo = sb("xt_lo", [P, KC, GROUP], FP32R)
        xn = sb("xn", [P, SUB, H])
        acc = sb("acc", [P, 2, SUB, H])
        h = sb("h", [P, R, N])
        hs_hi = sb("hs_hi", [P, R, N], FP32R)
        hs_lo = sb("hs_lo", [P, R, N], FP32R)
        mag = sb("mag", [P, R, N])
        top = sb("top", [P, 2, N])
        first = sb("first", [P, 2, N], BF16)
        both = sb("both", [P, 2, N], BF16)
        split = sb("split", [P, 2, N], BF16)
        keep = sb("keep", [P, R, N], BF16)
        ident = sb("ident", [P, P])
        stats = sb("stats", [P, SUB, 6])
        moments = sb("moments", [P, SUB, 2])
        shifted = sb("shifted", [P, SUB])
        rstd = sb("rstd", [P, SUB])
        power = sb("power", [P, SUB])
        eps = sb("eps", [P, SUB])

        gu = ctx.enter_context(nc.psum_tensor(f"{tag}_gu", [P, 2, 2, N], FP32))
        y = ctx.enter_context(nc.psum_tensor(f"{tag}_y", [P, SUB, H], FP32))

        ident_loaded = sem("ident_loaded")
        stage_loaded = [sem("stage_loaded0"), sem("stage_loaded1")]
        xn_loaded = sem("xn_loaded")
        acc_loaded = [sem("acc_loaded0"), sem("acc_loaded1")]
        acc_stored = [sem("acc_stored0"), sem("acc_stored1")]
        w_hi_done = sem("w_hi_done")
        w_lo_done = sem("w_lo_done")
        stats_done = sem("stats_done")
        power_set = sem("power_set")
        shift_done = sem("shift_done")
        rstd_done = sem("rstd_done")
        xn_done = sem("xn_done")
        xt_turned = sem("xt_turned")
        xt_hi_done = sem("xt_hi_done")
        xt_lo_done = sem("xt_lo_done")
        gu_done = sem("gu_done")
        silu_done = sem("silu_done")
        h_done = sem("h_done")
        mag_done = sem("mag_done")
        mask_step = sem("mask_step")
        masked = sem("masked")
        hs_hi_done = sem("hs_hi_done")
        hs_lo_done = sem("hs_lo_done")
        down_done = sem("down_done")
        y_added = sem("y_added")

        even, odd = mag[:, 0:R:2, :], mag[:, 1:R:2, :]
        def pieces(u):
            b, half = u // 2, u % 2
            start = b * QUARTERS + (0 if half == 0 else 2)
            gaps = (0, 1) if half == 0 else (0, 1, 2, 2)
            return [(g, start + k) for k, g in enumerate(gaps)]

        def piece_views(q, b):
            kind, part = q // 2, q % 2
            w = [w_hi[:, b, kind, :], w_lo[:, b, kind, :]]
            if kind < 2:
                dst = [v.rearrange("p (k r c) -> p k r c", k=KC, r=R)[:, 2 * part:2 * part + 2] for v in w]
                return dst, lambda s: s.rearrange("p k (c r) -> p k r c", r=R)
            dst = [v.rearrange("p (r n) -> p r n", r=R)[:, 2 * part:2 * part + 2, :] for v in w]
            return dst, lambda s: s

        def turned_tile(count, t):
            bank = y[:, t, :] if isinstance(count, int) and SUB <= count < 2 * SUB else gu[:, t // 2, t % 2, :]
            return bank.rearrange("p (k c) -> p k c", k=KC)

        def last_units(last):
            return UNITS - 2 if last else UNITS

        def loop(eng, body):
            body(0, True, False)
            if GROUPS > 2:
                with eng.Fori(1, GROUPS - 1) as g:
                    body(g, False, False)
            body(GROUPS - 1, False, True)

        block = ctx.enter_context(nc.Block())

        @block.sync
        def _(sync):
            def load_piece(g, n):
                block_of, q = n // QUARTERS % BLOCKS, n % QUARTERS
                kind, part = q // 2, q % 2
                count = g * (BLOCKS * QUARTERS) + n
                if n >= 2:
                    sync.wait_ge(w_lo_done, count - 1)
                if kind < 2:
                    src = (w_gate, w_up)[kind].rearrange("(k p) i -> p k i", p=P)
                    src = src[:, 2 * part:2 * part + 2, block_of * N:(block_of + 1) * N]
                else:
                    src = w_down.rearrange("(b p r) n -> b p r n", p=P, r=R)[block_of, :, 2 * part:2 * part + 2, :]
                sync.dma_start(stage[:, n % 2], src).then_inc(stage_loaded[n % 2], 16)

            def rows(g, half):
                return bass.ds(g * GROUP + half * N, N)

            def tiles(dram, g, half):
                return dram[rows(g, half), :].rearrange("(t p) n -> p t n", p=P)

            def store(g, half):
                sync.wait_ge(y_added, (g * UNITS + UNITS - 1 + half) * SUB)
                sync.dma_start(tiles(x_out, g, half), acc[:, half]).then_inc(acc_stored[half], 16)

            def reload(g, half):
                sync.wait_ge(acc_stored[half], g * 16)
                sync.dma_start(acc[:, half], tiles(x_in, g, half)).then_inc(acc_loaded[half], 16)

            sync.dma_start(xn[:], tiles(x_in, 0, 0)).then_inc(xn_loaded, 16)
            sync.dma_start(ident[:], ident_dram).then_inc(ident_loaded, 16)
            for n in range(4):
                load_piece(0, n)
            sync.wait_ge(xt_turned, SUB)
            sync.dma_start(xn[:], tiles(x_in, 0, 1)).then_inc(xn_loaded, 16)
            for n in range(4, QUARTERS):
                load_piece(0, n)
            for n in range(2):
                load_piece(0, QUARTERS + n)
            for half in range(2):
                sync.dma_start(acc[:, half], tiles(x_in, 0, half)).then_inc(acc_loaded[half], 16)

            def body(g, first, last):
                end = QUARTERS * (BLOCKS - 1) if last else QUARTERS * BLOCKS + 2
                for u in range(UNITS):
                    for _, c in pieces(u):
                        if c + 2 < end:
                            load_piece(g, QUARTERS + c + 2)
                    if u == 0 and not first:
                        store(g - 1, 1)
                        reload(g, 1)
                    if u == UNITS - 3 and not last:
                        sync.wait_ge(xt_turned, g * 2 * SUB + 2 * SUB)
                        sync.dma_start(xn[:], tiles(x_in, g + 1, 0)).then_inc(xn_loaded, 16)
                if not last:
                    sync.wait_ge(xt_turned, g * 2 * SUB + 3 * SUB)
                    sync.dma_start(xn[:], tiles(x_in, g + 1, 1)).then_inc(xn_loaded, 16)
                store(g, 0)
                if not last:
                    reload(g + 1, 0)

            loop(sync, body)
            store(GROUPS - 1, 1)
            for half in range(2):
                sync.wait_ge(acc_stored[half], GROUPS * 16)

        @block.gpsimd
        def _(pool):
            pool.memset(power[:], -0.5).then_inc(power_set, 1)
            pool.memset(eps[:], EPS).then_inc(power_set, 1)
            pool.wait_ge(power_set, 2)
            with pool.Fori(0, 2 * GROUPS) as i:
                pool.wait_ge(stats_done, (i + 1) * SUB)
                pool.tensor_tensor(shifted[:], moments[:, :, 1], eps[:], ALU.add).then_inc(shift_done, 1)
                pool.wait_ge(shift_done, i + 1)
                pool.tensor_tensor(rstd[:], shifted[:], power[:], ALU.pow).then_inc(rstd_done, 1)

        @block.scalar
        def _(act):
            def split_piece(g, n):
                q, b = n % QUARTERS, n // QUARTERS % 2
                count = g * (BLOCKS * QUARTERS) + n
                act.wait_ge(stage_loaded[n % 2], (g * (BLOCKS * QUARTERS // 2) + n // 2 + 1) * 16)
                dst, view = piece_views(q, b)
                act.activation(dst[0], view(stage[:, n % 2]), ACT.Copy).then_inc(w_hi_done, 1)

            def tile_hi(count, half, t):
                act.wait_ge(xt_turned, count + 1)
                at = half * N + t * P
                act.activation(xt_hi[:, :, at:at + P], turned_tile(count, t),
                               ACT.Copy).then_inc(xt_hi_done, 1)

            for n in range(2):
                split_piece(0, n)
            for t in range(SUB):
                tile_hi(t, 0, t)
            for n in range(2, QUARTERS):
                split_piece(0, n)

            def body(g, first, last):
                for u in range(UNITS):
                    unit = g * UNITS + u
                    splits = pieces(u) if u < last_units(last) else []
                    for r in range(R):
                        act.wait_ge(gu_done, unit * R + r + 1)
                        if not (first and u == 0):
                            act.wait_ge(hs_lo_done, unit * R - R + r + 1)
                        act.activation(h[:, r, :], gu[:, r % 2, 0, :], ACT.Silu).then_inc(silu_done, 1)
                        for gap, c in splits:
                            if gap == r:
                                if not (first and u < 2):
                                    act.wait_ge(gu_done if c % QUARTERS < 4 else down_done, (g * UNITS + u - u % 2) * R)
                                split_piece(g, QUARTERS + c)
                        if first and u == 0 and r == 1:
                            for t in range(SUB):
                                tile_hi(SUB + t, 1, t)
                        if r >= 2:
                            pair = r - 2
                            act.wait_ge(h_done, unit * R + 2 * pair + 2)
                            act.activation(mag[:, 2 * pair:2 * pair + 2, :], h[:, 2 * pair:2 * pair + 2, :],
                                           ACT.Abs).then_inc(mag_done, 1)
                    if u == 0 and not first:
                        for t in range(SUB):
                            tile_hi(g * 2 * SUB + SUB + t, 1, t)
                    if u == UNITS - 1 and not last:
                        for t in range(SUB):
                            tile_hi(g * 2 * SUB + 2 * SUB + t, 0, t)
                    for r in range(R):
                        act.wait_ge(masked, unit * R + r + 1)
                        if not (first and u == 0):
                            act.wait_ge(down_done, unit * R - R + r + 1)
                        act.activation(hs_hi[:, r, :], h[:, r, :], ACT.Copy).then_inc(hs_hi_done, 1)

            loop(act, body)

        @block.vector
        def _(dve):
            def split_piece(g, n):
                q, b = n % QUARTERS, n // QUARTERS % 2
                dst, view = piece_views(q, b)
                dve.wait_ge(w_hi_done, g * (BLOCKS * QUARTERS) + n + 1)
                dve.tensor_tensor(dst[1], view(stage[:, n % 2]), dst[0].bitcast(FP32),
                                  ALU.subtract).then_inc(w_lo_done, 1)

            def tile_lo(count, half, t):
                dve.wait_ge(xt_hi_done, count + 1)
                at = half * N + t * P
                dve.tensor_tensor(xt_lo[:, :, at:at + P], turned_tile(count, t),
                                  xt_hi[:, :, at:at + P].bitcast(FP32), ALU.subtract).then_inc(xt_lo_done, 1)

            def tile_stats(k):
                dve.wait_ge(xn_loaded, (k + 1) * 16)
                for t in range(SUB):
                    dve.bn_stats(stats[:, t, :], xn[:, t, :])
                dve.drain()
                for t in range(SUB):
                    dve.bn_aggr(moments[:, t, :], stats[:, t, :]).then_inc(stats_done, 1)

            def tile_norm(k):
                dve.wait_ge(rstd_done, k + 1)
                for t in range(SUB):
                    dve.tensor_scalar(xn[:, t, :], xn[:, t, :], moments[:, t, 0:1], rstd[:, t:t + 1],
                                      ALU.subtract, ALU.mult).then_inc(xn_done, 1)

            def add_block(g, u):
                half = u % 2
                dve.wait_ge(down_done, (g * UNITS + u + 1) * R)
                if u < 2:
                    dve.wait_ge(acc_loaded[half], (g + 1) * 16)
                else:
                    dve.wait_ge(y_added, (g * UNITS + u - 1) * SUB)
                for t in range(SUB):
                    dve.scalar_tensor_tensor(acc[:, half, t, :], y[:, t, :], 0.5, acc[:, half, t, :],
                                             ALU.mult, ALU.add).then_inc(y_added, 1)

            def compare(unit):
                step = unit * STEPS
                dve.wait_ge(mag_done, unit * 2 + 2)
                dve.tensor_tensor(first[:], even, odd, ALU.is_ge).then_inc(mask_step, 1)
                dve.tensor_tensor(top[:], even, odd, ALU.max).then_inc(mask_step, 1)
                dve.wait_ge(mask_step, step + 2)
                dve.tensor_tensor(even, even, odd, ALU.min).then_inc(mask_step, 1)
                dve.wait_ge(mask_step, step + 3)
                dve.tensor_tensor(both[:, 0, :], mag[:, 0, :], top[:, 1, :], ALU.is_ge).then_inc(mask_step, 1)
                dve.tensor_tensor(both[:, 1, :], mag[:, 2, :], top[:, 0, :], ALU.is_gt).then_inc(mask_step, 1)

            def choose(unit):
                step = unit * STEPS
                dve.wait_ge(mask_step, step + 5)
                dve.tensor_scalar(split[:, 0, :], both[:, 1, :], -1.0, 1.0, ALU.mult, ALU.add).then_inc(mask_step, 1)
                dve.tensor_scalar(split[:, 1, :], both[:, 0, :], -1.0, 1.0, ALU.mult, ALU.add).then_inc(mask_step, 1)
                dve.wait_ge(mask_step, step + 7)
                dve.tensor_tensor(keep[:, 0:R:2, :], first[:], split[:], ALU.mult).then_inc(mask_step, 1)
                dve.wait_ge(mask_step, step + 8)
                dve.tensor_tensor(keep[:, 1:R:2, :], split[:], keep[:, 0:R:2, :], ALU.subtract).then_inc(mask_step, 1)
                dve.wait_ge(mask_step, step + 9)
                pairs = keep[:].rearrange("p (a e) n -> p a e n", e=2)
                dve.tensor_tensor(pairs, pairs, both[:].unsqueeze(2).broadcast_to((P, 2, 2, N)),
                                  ALU.max).then_inc(mask_step, 1)

            def apply(unit):
                dve.wait_ge(mask_step, unit * STEPS + STEPS)
                for r in range(R):
                    dve.tensor_tensor(h[:, r, :], h[:, r, :], keep[:, r, :], ALU.mult).then_inc(masked, 1)
                for r in range(R):
                    dve.wait_ge(hs_hi_done, unit * R + r + 1)
                    dve.tensor_tensor(hs_lo[:, r, :], h[:, r, :], hs_hi[:, r, :].bitcast(FP32),
                                      ALU.subtract).then_inc(hs_lo_done, 1)

            tile_stats(0)
            for n in range(2):
                split_piece(0, n)
            tile_norm(0)
            for t in range(SUB):
                tile_lo(t, 0, t)
            for n in range(2, 4):
                split_piece(0, n)
            tile_stats(1)
            for n in range(4, QUARTERS):
                split_piece(0, n)
            tile_norm(1)

            def body(g, first, last):
                for u in range(UNITS):
                    unit = g * UNITS + u
                    splits = pieces(u) if u < last_units(last) else []
                    for r in range(R):
                        dve.wait_ge(silu_done, unit * R + r + 1)
                        dve.tensor_tensor(h[:, r, :], h[:, r, :], gu[:, r % 2, 1, :], ALU.mult).then_inc(h_done, 1)
                        for gap, c in splits:
                            if gap == r:
                                split_piece(g, QUARTERS + c)
                        if first and u == 0 and r == 1:
                            for t in range(SUB):
                                tile_lo(SUB + t, 1, t)
                        if u == 0 and r == 0 and not first:
                            tile_stats(2 * g + 1)
                        if u == 0 and r == 1 and not first:
                            tile_norm(2 * g + 1)
                        if u == UNITS - 2 and r == 2 and not last:
                            tile_stats(2 * g + 2)
                        if u == UNITS - 1 and r == 1 and not last:
                            tile_norm(2 * g + 2)
                    compare(unit)
                    if u == 0 and not first:
                        for t in range(SUB):
                            tile_lo(g * 2 * SUB + SUB + t, 1, t)
                    if u == UNITS - 1 and not last:
                        for t in range(SUB):
                            tile_lo(g * 2 * SUB + 2 * SUB + t, 0, t)
                    choose(unit)
                    apply(unit)
                    if u:
                        add_block(g, u - 1)
                    elif not first:
                        add_block(g - 1, UNITS - 1)

            loop(dve, body)
            add_block(GROUPS - 1, UNITS - 1)

        @block.tensor
        def _(pe):
            def gate_up(g, u, r, first):
                unit, b = g * UNITS + u, u // 2 % 2
                half = u % 2
                if r == 0:
                    if u < 2:
                        pe.wait_ge(xt_lo_done, g * 2 * SUB + (u + 1) * SUB)
                    if half == 0:
                        pe.wait_ge(w_lo_done, g * (BLOCKS * QUARTERS) + u // 2 * QUARTERS + 4)
                if not (first and u == 0 and r < 2):
                    pe.wait_ge(h_done, unit * R + r - 1)
                for kind in range(2):
                    whi = w_hi[:, b, kind, :].rearrange("p (k r c) -> p k r c", k=KC, r=R)
                    wlo = w_lo[:, b, kind, :].rearrange("p (k r c) -> p k r c", k=KC, r=R)
                    for k in range(KC):
                        xh = xt_hi[:, k, half * N:(half + 1) * N]
                        xl = xt_lo[:, k, half * N:(half + 1) * N]
                        for i, (w, x) in enumerate(((whi, xh), (whi, xl), (wlo, xh))):
                            last = nc.tensor.matmul(gu[:, r % 2, kind, :], w[:, k, r, :], x,
                                                    start=k == 0 and i == 0, stop=k == KC - 1 and i == 2)
                last.then_inc(gu_done, 1)

            def down(g, u, turned=None):
                unit, b = g * UNITS + u, u // 2 % 2
                if not (isinstance(unit, int) and unit == 0):
                    pe.wait_ge(y_added, unit * SUB)
                if u % 2 == 0:
                    pe.wait_ge(w_lo_done, g * (BLOCKS * QUARTERS) + u // 2 * QUARTERS + 6)
                for r in range(R):
                    if r == 1 and turned is not None:
                        turn_half(turned, unit + 1)
                    pe.wait_ge(hs_lo_done, unit * R + r + 1)
                    wh = w_hi[:, b, 2, r * N:(r + 1) * N]
                    wl = w_lo[:, b, 2, r * N:(r + 1) * N]
                    for t in range(SUB):
                        at = slice(t * P, (t + 1) * P)
                        for i, (x, w) in enumerate(((hs_hi, wh), (hs_hi, wl), (hs_lo, wh))):
                            last = nc.tensor.matmul(y[:, t, :], x[:, r, at], w, start=r == 0 and i == 0,
                                                    stop=r == R - 1 and i == 2)
                    last.then_inc(down_done, 1)

            def turn(count, t):
                pe.wait_ge(xn_done, count + 1)
                for k in range(KC):
                    last = nc.tensor.transpose(turned_tile(count, t)[:, k, :], xn[:, t, k * P:(k + 1) * P],
                                               ident[:])
                last.then_inc(xt_turned, 1)

            def turn_half(count, unit):
                pe.wait_ge(h_done, (unit + 1) * R)
                for t in range(SUB):
                    turn(count + t, t)

            pe.wait_ge(ident_loaded, 16)
            for t in range(SUB):
                turn(t, t)

            def body(g, first, last):
                for u in range(UNITS):
                    for r in range(R):
                        gate_up(g, u, r, first)
                        if first and u == 0 and r == 1:
                            for t in range(SUB):
                                turn(SUB + t, t)
                    if u == 0:
                        if not first:
                            down(g - 1, UNITS - 1, g * 2 * SUB + SUB)
                    elif u == UNITS - 1 and not last:
                        down(g, u - 1, g * 2 * SUB + 2 * SUB)
                    else:
                        down(g, u - 1)

            loop(pe, body)
            down(GROUPS - 1, UNITS - 1)


def qkv_phase(nc, ident_dram, cos_dram, sin_dram, x_in, w_q, w_k, w_v, qk_hi_out, qk_lo_out, v_out, seq):
    TOKENS, H = x_in.shape
    KC = H // P
    TILES = seq // P
    SEQS = TOKENS // seq
    DQ, DK = w_q.shape[1], w_k.shape[1]
    QK = DQ + DK
    ALL = QK + DK
    CH = QK // P
    KVH = DK // HEAD
    VW = 3 * (P // 2)

    ctx = ExitStack()
    with ctx:
        def sb(name, shape, dtype=FP32):
            return ctx.enter_context(nc.sbuf_tensor(f"qkv_{name}", shape, dtype))

        def ps(name, shape):
            return ctx.enter_context(nc.psum_tensor(f"qkv_{name}", shape, FP32))

        def sem(name):
            return ctx.enter_context(nc.semaphore(f"qkv_{name}"))

        w = sb("w", [P, KC, ALL])
        w_hi = sb("w_hi", [P, KC, ALL], FP32R)
        w_lo = sb("w_lo", [P, KC, ALL], FP32R)
        cos = sb("cos", [P, TILES, QK])
        sin = sb("sin", [P, TILES, QK])
        ident = sb("ident", [P, P])
        x = sb("x", [P, TILES, H])
        xn = sb("xn", [P, TILES, H])
        xt_hi = sb("xt_hi", [P, 2, KC, P], FP32R)
        xt_lo = sb("xt_lo", [P, 2, KC, P], FP32R)
        rot = sb("rot", [P, 2, QK])
        cross = sb("cross", [P, 2, QK])
        qk_hi = sb("qk_hi", [P, CH, seq], FP32R)
        qk_lo = sb("qk_lo", [P, CH, seq], FP32R)
        v = sb("v", [P, TILES, KVH * VW], FP32R)
        stats = sb("stats", [P, TILES, 6])
        moments = sb("moments", [P, TILES, 2])
        shifted = sb("shifted", [P, TILES])
        rstd = sb("rstd", [P, TILES])
        power = sb("power", [P, TILES])
        eps = sb("eps", [P, TILES])

        xbank = ps("xbank", [P, 2, KC * P])
        proj = ps("proj", [P, 2, 2 * N])
        qbank = ps("qbank", [P, 2 * N])

        ident_loaded = sem("ident_loaded")
        table_loaded = [sem(f"table_loaded{t}") for t in range(TILES)]
        w_loaded = sem("w_loaded")
        x_loaded = sem("x_loaded")
        w_hi_done = sem("w_hi_done")
        w_lo_done = sem("w_lo_done")
        v_cleared = sem("v_cleared")
        stats_done = sem("stats_done")
        power_set = sem("power_set")
        shift_done = sem("shift_done")
        rstd_done = sem("rstd_done")
        xn_done = sem("xn_done")
        xt_turned = sem("xt_turned")
        xt_hi_done = sem("xt_hi_done")
        xt_lo_done = sem("xt_lo_done")
        proj_done = sem("proj_done")
        cos_done = sem("cos_done")
        cross_done = sem("cross_done")
        rot_done = sem("rot_done")
        v_hi_done = sem("v_hi_done")
        v_lo_done = sem("v_lo_done")
        qk_turned = sem("qk_turned")
        qk_hi_done = sem("qk_hi_done")
        qk_lo_done = sem("qk_lo_done")
        v_stored = [sem(f"v_stored{t}") for t in range(TILES)]
        qk_stored = [sem(f"qk_stored{t}") for t in range(TILES)]

        BEFORE = [("X", 0), ("X", 1)]
        AFTER = [("R", -1)]

        def order(first, load, more):
            found = []
            for t in range(TILES):
                if load and t == 2:
                    found.append(("L", t))
                found.append(("J", t))
                if more or t + 2 < TILES:
                    found.append(("X", t + 2))
                if not (first and t == 0):
                    found.append(("R", t - 1))
            return found

        def value_columns(t, part):
            pairs = v[:, t, :].rearrange("p (j w) -> p j w", w=2 * VW)
            at = part * (P // 2)
            return [pairs[:, :, at + e * (VW + HEAD):at + e * (VW + HEAD) + HEAD] for e in range(2)]

        def loop(eng, body):
            body(0, BEFORE)
            body(0, order(True, True, True))
            body(1, order(False, True, True))
            with eng.Fori(2, SEQS - 2) as s:
                body(s, order(False, True, True))
            body(SEQS - 2, order(False, False, True))
            body(SEQS - 1, order(False, False, False))
            body(SEQS, AFTER)

        def wait(eng, semaphore, count):
            if not (isinstance(count, int) and count <= 0):
                eng.wait_ge(semaphore, count)

        block = ctx.enter_context(nc.Block())

        @block.sync
        def _(sync):
            def tiles(dram, s):
                return dram[bass.ds(s * seq, seq), :].rearrange("(t p) n -> p t n", p=P)

            sync.dma_start(x[:], tiles(x_in, 0)).then_inc(x_loaded, 16)
            sync.dma_start(ident[:], ident_dram).then_inc(ident_loaded, 16)
            at = 0
            for dram in (w_q, w_k, w_v):
                width = dram.shape[1]
                sync.dma_start(w[:, :, at:at + width], dram.rearrange("(k p) n -> p k n", p=P)).then_inc(w_loaded, 16)
                at += width
            sync.wait_ge(xn_done, TILES)
            sync.dma_start(x[:], tiles(x_in, 1)).then_inc(x_loaded, 16)
            for t in range(TILES):
                for table, dram in ((cos, cos_dram), (sin, sin_dram)):
                    sync.dma_start(table[:, t, :], dram[t * P:(t + 1) * P, :]).then_inc(table_loaded[t], 16)

            def body(s, steps):
                for step, t in steps:
                    if step == "L":
                        sync.wait_ge(xn_done, (s + 2) * TILES)
                        sync.dma_start(x[:], tiles(x_in, s + 2)).then_inc(x_loaded, 16)
                    if step == "J":
                        sync.wait_ge(v_lo_done, 2 * (s * TILES + t + 1))
                        sync.dma_start(v_out[bass.ds(s, 1), :, t, :].rearrange("s p n -> p (s n)"),
                                       v[:, t, :].bitcast(FP32)).then_inc(v_stored[t], 16)
                    if step == "R":
                        sync.wait_ge(qk_lo_done, s * TILES + t + 1)
                        at = t % TILES
                        cols = slice(at * P, (at + 1) * P)
                        for dram, part in ((qk_hi_out, qk_hi), (qk_lo_out, qk_lo)):
                            sync.dma_start(dram[bass.ds(s - (t < 0), 1), :, :, cols].rearrange("s p c n -> (s p) c n"),
                                           part[:, :, cols].bitcast(FP32)).then_inc(qk_stored[at], 16)

            loop(sync, body)
            for t in range(TILES):
                sync.wait_ge(v_stored[t], SEQS * 16)
                sync.wait_ge(qk_stored[t], SEQS * 32)

        @block.gpsimd
        def _(pool):
            pool.memset(power[:], -0.5).then_inc(power_set, 1)
            pool.memset(eps[:], EPS).then_inc(power_set, 1)
            pool.memset(v[:].bitcast(FP32), 0.0).then_inc(v_cleared, 1)
            pool.wait_ge(v_cleared, 1)
            for t in range(TILES):
                for ones in value_columns(t, 1):
                    pool.memset(ones.bitcast(FP32), 1.0).then_inc(v_cleared, 1)
            pool.wait_ge(power_set, 2)

            def inverse_deviation(s):
                pool.wait_ge(stats_done, (s + 1) * TILES)
                pool.tensor_tensor(shifted[:], moments[:, :, 1], eps[:], ALU.add).then_inc(shift_done, 1)
                pool.wait_ge(shift_done, s + 1)
                pool.tensor_tensor(rstd[:], shifted[:], power[:], ALU.pow).then_inc(rstd_done, 1)

            inverse_deviation(0)

            def body(s, steps):
                for step, t in steps:
                    tile = s * TILES + t
                    if step == "J":
                        pool.wait_ge(cos_done, tile + 1)
                        pool.wait_ge(cross_done, 2 * tile + 2)
                        pool.tensor_tensor(rot[:, t % 2, :], rot[:, t % 2, :], cross[:, t % 2, :],
                                           ALU.add).then_inc(rot_done, 1)
                    if step == "J" and t == 0 and ("X", TILES) in steps:
                        inverse_deviation(s + 1)

            loop(pool, body)

        @block.scalar
        def _(act):
            act.wait_ge(w_loaded, 48)
            for k in range(KC):
                act.activation(w_hi[:, k, :], w[:, k, :], ACT.Copy).then_inc(w_hi_done, 1)
            act.wait_ge(v_cleared, 1 + 2 * TILES)

            def body(s, steps):
                for step, t in steps:
                    tile = s * TILES + t
                    if step == "X":
                        act.wait_ge(xt_turned, tile + 1)
                        wait(act, proj_done, tile - 1)
                        act.activation(xt_hi[:, t % 2], xbank[:, t % 2, :].rearrange("p (k c) -> p k c", k=KC),
                                       ACT.Copy).then_inc(xt_hi_done, 1)
                    if step == "J":
                        act.wait_ge(proj_done, tile + 1)
                        wait(act, v_stored[t], s * 16)
                        values = proj[:, t % 2, QK:ALL].rearrange("p (j e d) -> p j e d", e=2, d=HEAD)
                        for e, out in enumerate(value_columns(t, 0)):
                            act.activation(out, values[:, :, e, :], ACT.Copy).then_inc(v_hi_done, 1)
                    if step == "R":
                        act.wait_ge(qk_turned, tile + 1)
                        at = t % TILES
                        wait(act, qk_stored[at], (s - (t < 0)) * 32)
                        act.activation(qk_hi[:, :, at * P:(at + 1) * P], qbank[:, 0:QK].rearrange("p (c n) -> p c n", n=P),
                                       ACT.Copy).then_inc(qk_hi_done, 1)

            loop(act, body)

        @block.vector
        def _(dve):
            def tile_stats(s):
                dve.wait_ge(x_loaded, (s + 1) * 16)
                for t in range(TILES):
                    dve.bn_stats(stats[:, t, :], x[:, t, :])
                dve.drain()
                for t in range(TILES):
                    dve.bn_aggr(moments[:, t, :], stats[:, t, :]).then_inc(stats_done, 1)

            def tile_norm(s):
                dve.wait_ge(rstd_done, s + 1)
                wait(dve, xt_turned, s * TILES)
                for t in range(TILES):
                    dve.tensor_scalar(xn[:, t, :], x[:, t, :], moments[:, t, 0:1], rstd[:, t:t + 1],
                                      ALU.subtract, ALU.mult).then_inc(xn_done, 1)

            def w_low(k):
                dve.wait_ge(w_hi_done, k + 1)
                dve.tensor_tensor(w_lo[:, k, :], w[:, k, :], w_hi[:, k, :].bitcast(FP32),
                                  ALU.subtract).then_inc(w_lo_done, 1)

            tile_stats(0)
            tile_norm(0)
            for k in range(KC):
                w_low(k)

            def body(s, steps):
                first = ("R", -1) not in steps
                for step, t in steps:
                    tile = s * TILES + t
                    if step == "X":
                        dve.wait_ge(xt_hi_done, tile + 1)
                        dve.tensor_tensor(xt_lo[:, t % 2], xbank[:, t % 2, :].rearrange("p (k c) -> p k c", k=KC),
                                          xt_hi[:, t % 2].bitcast(FP32), ALU.subtract).then_inc(xt_lo_done, 1)
                    if step == "J":
                        if t == 2 and ("X", TILES) in steps:
                            tile_norm(s + 1)
                        both = proj[:, t % 2, 0:QK]
                        if first:
                            dve.wait_ge(table_loaded[t], 32)
                        dve.wait_ge(v_hi_done, 2 * tile + 2)
                        wait(dve, qk_turned, tile - 1)
                        dve.tensor_tensor(rot[:, t % 2, :], both, cos[:, t, :], ALU.mult).then_inc(cos_done, 1)
                        dve.tensor_tensor(cross[:, t % 2, 0:QK:2], both[:, 1:QK:2], sin[:, t, 0:QK:2],
                                          ALU.mult).then_inc(cross_done, 1)
                        dve.tensor_tensor(cross[:, t % 2, 1:QK:2], both[:, 0:QK:2], sin[:, t, 1:QK:2],
                                          ALU.mult).then_inc(cross_done, 1)
                        for e in range(2):
                            values = proj[:, t % 2, QK:ALL].rearrange("p (j e d) -> p j e d", e=2, d=HEAD)
                            dve.tensor_tensor(value_columns(t, 2)[e], values[:, :, e, :],
                                              value_columns(t, 0)[e].bitcast(FP32),
                                              ALU.subtract).then_inc(v_lo_done, 1)
                        if t == 0 and ("X", TILES) in steps:
                            tile_stats(s + 1)
                    if step == "R":
                        dve.wait_ge(qk_hi_done, tile + 1)
                        at = t % TILES
                        cols = slice(at * P, (at + 1) * P)
                        dve.tensor_tensor(qk_lo[:, :, cols], qbank[:, 0:QK].rearrange("p (c n) -> p c n", n=P),
                                          qk_hi[:, :, cols].bitcast(FP32), ALU.subtract).then_inc(qk_lo_done, 1)

            loop(dve, body)

        @block.tensor
        def _(pe):
            pe.wait_ge(ident_loaded, 16)

            def body(s, steps):
                for step, t in steps:
                    tile = s * TILES + t
                    if step == "X":
                        pe.wait_ge(xn_done, tile + 1)
                        wait(pe, xt_lo_done, tile - 1)
                        for k in range(KC):
                            last_one = nc.tensor.transpose(xbank[:, t % 2, k * P:(k + 1) * P],
                                                           xn[:, t % TILES, k * P:(k + 1) * P], ident[:])
                        last_one.then_inc(xt_turned, 1)
                    if step == "J":
                        pe.wait_ge(xt_lo_done, tile + 1)
                        if t == 0:
                            pe.wait_ge(w_lo_done, KC)
                        wait(pe, v_lo_done, 2 * (tile - 1))
                        for at, width in ((0, N), (N, ALL - N)):
                            for k in range(KC):
                                for i, (xx, ww) in enumerate(((xt_hi, w_hi), (xt_hi, w_lo), (xt_lo, w_hi))):
                                    last_one = nc.tensor.matmul(proj[:, t % 2, at:at + width], xx[:, t % 2, k, :],
                                                                ww[:, k, at:at + width], start=k == 0 and i == 0,
                                                                stop=k == KC - 1 and i == 2)
                        last_one.then_inc(proj_done, 1)
                    if step == "R":
                        pe.wait_ge(rot_done, tile + 1)
                        wait(pe, qk_lo_done, tile)
                        for c in range(CH):
                            last_one = nc.tensor.transpose(qbank[:, c * P:(c + 1) * P],
                                                           rot[:, t % 2, c * P:(c + 1) * P], ident[:])
                        last_one.then_inc(qk_turned, 1)

            loop(pe, body)


def attention_phase(nc, ident_dram, qk_hi, qk_lo, v_in, w_o, x_in, x_out, seq):
    TOKENS, H = x_in.shape
    TILES = seq // P
    SEQS = TOKENS // seq
    CHUNKS = H // P
    HEADS = P // HEAD
    PLANES = 3
    AT_MAX = PLANES * HEAD
    HALVES = TILES // 2
    UNITS = HEADS * HALVES
    PAIR = UNITS // 2
    TURN = 2
    TURNS = SEQS // TURN
    TURN_CHUNKS = TURN * CHUNKS
    TURN_UNITS = TURN_CHUNKS * UNITS
    RING = 4
    VW = 3 * (P // 2)

    ctx = ExitStack()
    with ctx:
        def sb(name, shape, dtype=FP32):
            return ctx.enter_context(nc.sbuf_tensor(f"attn_{name}", shape, dtype))

        def ps(name, shape):
            return ctx.enter_context(nc.psum_tensor(f"attn_{name}", shape, FP32))

        def sem(name):
            return ctx.enter_context(nc.semaphore(f"attn_{name}"))

        qk = sb("qk", [P, TURN, CHUNKS + 1, HEADS, seq], FP32R)
        v = sb("v", [P, TURN, TILES, HEADS * VW], FP32R)
        e = sb("e", [P, RING, 2, seq])
        p_hi = sb("p_hi", [P, RING, 2, seq], FP32R)
        p_lo = sb("p_lo", [P, RING, 2, seq], FP32R)
        w_hi = sb("w_hi", [P, CHUNKS, H], FP32R)
        w_lo = sb("w_lo", [P, CHUNKS, H], FP32R)
        x = sb("x", [P, TILES, H])
        o = sb("o", [P, seq])
        o_raw = sb("o_raw", [P, 2, seq])
        sums = sb("sums", [P, 2, seq])
        columns = sb("columns", [P, seq // HEAD, HEAD])
        inverse = sb("inverse", [P, seq // HEAD])
        o_hi = sb("o_hi", [P, CHUNKS, seq], FP32R)
        o_lo = sb("o_lo", [P, CHUNKS, seq], FP32R)
        neg_max = sb("neg_max", [P, 2, TILES, HEADS])
        max_parts = sb("max_parts", [P, TILES, 2, HEADS], FP32R)
        max_rows = sb("max_rows", [2 * HEADS, seq], FP32R)
        ident = sb("ident", [P, P])

        ring = ps("ring", [P, 2, seq])
        scores = ps("scores", [P, 2, 2, seq])
        out_t = ps("out_t", [P, 2, seq])

        ident_loaded = sem("ident_loaded")
        w_loaded = sem("w_loaded")
        qk_loaded = [sem("qk_loaded0"), sem("qk_loaded1")]
        queries_loaded = [sem("queries_loaded0"), sem("queries_loaded1")]
        v_loaded = [sem("v_loaded0"), sem("v_loaded1")]
        rows_loaded = sem("rows_loaded")
        x_loaded = sem("x_loaded")
        x_stored = sem("x_stored")
        ones_set = sem("ones_set")
        w_hi_done = sem("w_hi_done")
        w_lo_done = sem("w_lo_done")
        ring_written = sem("ring_written")
        ring_read = sem("ring_read")
        max_hi_done = sem("max_hi_done")
        max_lo_done = sem("max_lo_done")
        scores_done = sem("scores_done")
        exp_done = sem("exp_done")
        hi_done = sem("hi_done")
        lo_by_pool = sem("lo_by_pool")
        lo_by_dve = sem("lo_by_dve")
        pv_done = sem("pv_done")
        joined = sem("joined")
        columns_done = sem("columns_done")
        inverse_done = sem("inverse_done")
        rows_done = sem("rows_done")
        o_done = sem("o_done")
        o_hi_done = sem("o_hi_done")
        o_lo_done = sem("o_lo_done")

        DVE_LO = 3

        def lo_count(turn, unit):
            if unit % 4 == DVE_LO:
                return True, turn * (TURN_UNITS // 4) + unit // 4 + 1
            return False, turn * (TURN_UNITS // 4 * 3) + unit // 4 * 3 + unit % 4 + 1

        def wait(eng, semaphore, count):
            if not (isinstance(count, int) and count <= 0):
                eng.wait_ge(semaphore, count)

        def wait_lo(eng, turn, unit):
            by_dve, count = lo_count(turn, unit)
            wait(eng, lo_by_dve if by_dve else lo_by_pool, count)

        MAX_SPLIT, MAX_TURN = 1, 2
        AFTER_CHUNK = (("columns", 2), ("invert", 3), ("norm", 5), ("o_split", 7))
        OUT_AT = (0, 1, 3, 4)

        def order(first, last):
            found, slot = [], 0

            def add(step, index, k=0, uses=False):
                nonlocal slot
                found.append((step, index, k, slot))
                slot += uses

            for j in range(TURN_UNITS):
                g, u = divmod(j, UNITS)
                more = not (last and g >= TURN_CHUNKS - 2)
                if not (last and j + 4 >= TURN_UNITS):
                    add("scores", j + 4)
                if not (last and j + 3 >= TURN_UNITS):
                    add("exp", j + 3)
                next_chunk = not (last and g == TURN_CHUNKS - 1)
                if u == MAX_SPLIT and next_chunk:
                    add("max_split", g + 1)
                if u == MAX_TURN and next_chunk:
                    add("max_turn", g + 1, 0, True)
                if more:
                    add("max", g + 2, 2 * u, True)
                add("value", j, 0)
                for step, at in AFTER_CHUNK:
                    if u == at and not (first and g == 0):
                        add(step, g - 1)
                if more:
                    add("max", g + 2, 2 * u + 1, True)
                add("value", j, 1)
                if not (last and j + 3 >= TURN_UNITS):
                    add("high", j + 3)
                if not (last and j + 2 >= TURN_UNITS):
                    add("low", j + 2)
                if u == PAIR + 1 or (u == 1 and not (first and g == 0)):
                    add("join", j // PAIR - 1)
                if g % CHUNKS == 1 and not (first and g == 1) and u in OUT_AT:
                    add("out", g // CHUNKS, OUT_AT.index(u), True)
                if first and g == 1 and u < CHUNKS:
                    add("w_split", u)
            return found

        START = [("max", 0, k, k) for k in range(HEADS * TILES)]
        START += [("max_split", 0, 0, len(START)), ("max_turn", 0, 0, len(START))]
        AHEAD = [("scores", 0), ("scores", 1), ("exp", 0), ("high", 0), ("low", 0), ("scores", 2), ("exp", 1),
                 ("high", 1), ("low", 1), ("scores", 3), ("exp", 2), ("high", 2)]
        for k in range(HEADS * TILES):
            START.append(("max", 1, k, HEADS * TILES + 1 + k))
            if k >= HEADS * TILES // 2 - 2:
                START += [(step, unit, 0, 0) for step, unit in AHEAD[:2]]
                AHEAD = AHEAD[2:]
        END = [(step, -1, 0, 0) for step in ("join", "columns", "invert", "norm", "o_split")]
        END += [("out", 0, t, t) for t in range(TILES)]
        START_SLOTS = 2 * HEADS * TILES + 1
        TURN_SLOTS = TURN_CHUNKS * (HEADS * TILES + 1) + TURN * TILES

        def slots_before(turn, kind):
            if kind == "start":
                return 0
            if kind == "first":
                return START_SLOTS
            base = turn * TURN_SLOTS + START_SLOTS - TILES
            return base - (2 * HEADS * TILES + 1) if kind == "end" else base

        def parity(kind):
            return slots_before(0 if kind in ("start", "first") else TURNS if kind == "end" else 1, kind) % 2

        def loop(eng, body):
            body(0, START, "start")
            body(0, order(True, False), "first")
            if TURNS > 2:
                with eng.Fori(1, TURNS - 1) as turn:
                    body(turn, order(False, False), "middle")
            body(TURNS - 1, order(False, True), "last")
            body(TURNS, END, "end")

        block = ctx.enter_context(nc.Block())

        @block.sync
        def _(sync):
            def load_qk(s, b):
                for c in (CHUNKS, *range(CHUNKS)):
                    parts = (qk_hi, qk_hi, qk_lo) if c == CHUNKS else (qk_hi, qk_lo, qk_hi)
                    for plane, dram in enumerate(parts):
                        rows = slice(plane * HEAD, (plane + 1) * HEAD)
                        src = dram[bass.ds(s, 1), :, c, :].rearrange("s (i d) n -> (s d) i n", d=HEAD)
                        sync.dma_start(qk[rows, b, c, :, :].bitcast(FP32),
                                       src).then_inc((qk_loaded if c in (0, CHUNKS) else queries_loaded)[b], 16)

            def load_v(s, b):
                sync.dma_start(v[:, b].bitcast(FP32),
                               v_in[bass.ds(s, 1)].rearrange("s p t n -> (s p) t n")).then_inc(v_loaded[b], 16)

            def tiles(dram, s):
                return dram[bass.ds(s * seq, seq), :].rearrange("(t p) n -> p t n", p=P)

            sync.dma_start(ident[:], ident_dram).then_inc(ident_loaded, 16)
            load_qk(0, 0)
            load_v(0, 0)
            sync.dma_start(x[:], w_o.rearrange("(c p) n -> p c n", p=P)).then_inc(w_loaded, 16)

            def body(turn, steps, kind):
                base = slots_before(turn, kind)
                for step, index, k, slot in steps:
                    if step == "max_turn":
                        sync.wait_ge(ring_read, base + slot + 1)
                        nb, c = index // CHUNKS % TURN, index % CHUNKS
                        for part in range(2):
                            at = AT_MAX + part
                            sync.dma_start(qk[at:at + 1, nb, c, :, :].bitcast(FP32),
                                           max_rows[part * HEADS:(part + 1) * HEADS, :].bitcast(FP32)
                                           ).then_inc(rows_loaded, 16)
                        if kind == "start":
                            load_qk(1, 1)
                            load_v(1, 1)
                        elif index % CHUNKS == 1:
                            half = index // CHUNKS
                            s = turn * TURN + half
                            if (kind, half) not in (("first", 0), ("last", 1)):
                                sync.wait_ge(pv_done, s * (CHUNKS * UNITS))
                                load_qk(s + 1, (half + 1) % TURN)
                                load_v(s + 1, (half + 1) % TURN)
                    if step == "w_split" and index == CHUNKS - 1:
                        sync.wait_ge(w_lo_done, CHUNKS)
                        sync.dma_start(x[:], tiles(x_in, 0)).then_inc(x_loaded, 16)
                    if step == "out" and k == TILES - 1:
                        sync.wait_ge(ring_read, base + slot + 1)
                        s = turn * TURN + index
                        sync.dma_start(tiles(x_out, s - 1), x[:]).then_inc(x_stored, 16)
                        sync.wait_ge(x_stored, s * 16)
                        if kind != "end":
                            sync.dma_start(x[:], tiles(x_in, s)).then_inc(x_loaded, 16)

            loop(sync, body)

        @block.gpsimd
        def _(pool):
            for b in range(TURN):
                pool.memset(qk[AT_MAX:AT_MAX + 2, b, CHUNKS, :, :].bitcast(FP32), 1.0).then_inc(ones_set, 1)

            def body(turn, steps, kind):
                for step, unit, _, _ in steps:
                    if step == "low" and unit % 4 != DVE_LO:
                        pool.wait_ge(hi_done, turn * TURN_UNITS + unit + 1)
                        pool.tensor_tensor(p_lo[:, unit % RING], e[:, unit % RING], p_hi[:, unit % RING].bitcast(FP32),
                                           ALU.subtract).then_inc(lo_by_pool, 1)

            loop(pool, body)

        @block.scalar
        def _(act):
            def body(turn, steps, kind):
                base = slots_before(turn, kind)
                for step, index, k, slot in steps:
                    unit = turn * TURN_UNITS + index
                    if step == "exp":
                        act.wait_ge(scores_done, unit + 1)
                        wait_lo(act, turn, index - RING)
                        act.activation(e[:, index % RING], scores[:, index % 2], ACT.Exp).then_inc(exp_done, 1)
                    if step == "high":
                        act.wait_ge(exp_done, unit + 1)
                        wait(act, pv_done, unit - RING + 1)
                        act.activation(p_hi[:, index % RING], e[:, index % RING], ACT.Copy).then_inc(hi_done, 1)
                    if step == "join":
                        pair = turn * (TURN_UNITS // PAIR) + index
                        act.wait_ge(pv_done, pair * PAIR + PAIR)
                        if index % 2 == 0:
                            wait(act, o_done, turn * TURN_CHUNKS + index // 2 - 1)
                        rows = slice(index % 2 * (P // 2), (index % 2 + 1) * (P // 2))
                        for to, at in ((o_raw, 0), (sums, P // 2)):
                            act.activation(to[rows, index // 2 % 2, :], out_t[at:at + P // 2, index % 2, :],
                                           ACT.Copy).then_inc(joined, 1)
                    if step == "max_split":
                        act.wait_ge(ring_read, base + slot)
                        act.activation(max_parts[:, :, 0, :], neg_max[:, index % 2], ACT.Copy).then_inc(max_hi_done, 1)
                    if step == "o_split":
                        chunk = turn * TURN_CHUNKS + index
                        act.wait_ge(o_done, chunk + 1)
                        if index % CHUNKS == 0:
                            act.wait_ge(ring_read, base + slot)
                        act.activation(o_hi[:, index % CHUNKS, :], o[:], ACT.Copy).then_inc(o_hi_done, 1)
                    if step == "w_split":
                        act.wait_ge(w_loaded, 16)
                        act.activation(w_hi[:, index, :], x[:, index, :], ACT.Copy).then_inc(w_hi_done, 1)

            loop(act, body)

        @block.vector
        def _(dve):
            def body(turn, steps, kind):
                base = slots_before(turn, kind)
                for step, index, k, slot in steps:
                    unit = turn * TURN_UNITS + index
                    bank = (parity(kind) + slot) % 2
                    if step == "max":
                        i, t = k // TILES, k % TILES
                        dve.wait_ge(ring_written, base + slot + 1)
                        dve.tensor_reduce(neg_max[:, index % 2, t, i:i + 1], ring[:, bank, :], AX.X, ALU.max,
                                          negate=True).then_inc(ring_read, 1)
                    if step == "max_split":
                        chunk = turn * TURN_CHUNKS + index
                        dve.wait_ge(max_hi_done, chunk + 1)
                        dve.tensor_tensor(max_parts[:, :, 1, :], neg_max[:, index % 2],
                                          max_parts[:, :, 0, :].bitcast(FP32), ALU.subtract).then_inc(max_lo_done, 1)
                    if step == "max_turn":
                        chunk = turn * TURN_CHUNKS + index
                        dve.wait_ge(ring_written, base + slot + 1)
                        wait(dve, rows_loaded, chunk * 32)
                        dve.tensor_copy(max_rows[:], ring[0:2 * HEADS, bank, :]).then_inc(ring_read, 1)
                    if step == "low" and index % 4 == DVE_LO:
                        dve.wait_ge(hi_done, unit + 1)
                        dve.tensor_tensor(p_lo[:, index % RING], e[:, index % RING], p_hi[:, index % RING].bitcast(FP32),
                                          ALU.subtract).then_inc(lo_by_dve, 1)
                    chunk = turn * TURN_CHUNKS + index
                    if step == "columns":
                        dve.wait_ge(joined, chunk * 4 + 4)
                        dve.transpose(columns[:].rearrange("p b c -> p (b c)"), sums[:, index % 2]).then_inc(columns_done, 1)
                        dve.wait_ge(columns_done, chunk + 1)
                        dve.reciprocal(inverse[:], columns[:, :, 0]).then_inc(inverse_done, 1)
                    if step == "invert":
                        dve.wait_ge(inverse_done, chunk + 1)
                        dve.transpose(sums[:, index % 2].rearrange("p (b c) -> p b c", c=HEAD),
                                      inverse[:].unsqueeze(2).broadcast_to((P, seq // HEAD, HEAD))
                                      ).then_inc(rows_done, 1)
                    if step == "norm":
                        dve.wait_ge(rows_done, chunk + 1)
                        wait(dve, o_lo_done, chunk)
                        dve.tensor_tensor(o[:], o_raw[:, index % 2], sums[:, index % 2], ALU.mult).then_inc(o_done, 1)
                    if step == "o_split":
                        dve.wait_ge(o_hi_done, chunk + 1)
                        c = index % CHUNKS
                        dve.tensor_tensor(o_lo[:, c, :], o[:], o_hi[:, c, :].bitcast(FP32),
                                          ALU.subtract).then_inc(o_lo_done, 1)
                    if step == "out":
                        dve.wait_ge(ring_written, base + slot + 1)
                        if k == 0:
                            dve.wait_ge(x_loaded, (turn * TURN + index) * 16)
                        dve.tensor_tensor(x[:, k, :], x[:, k, :], ring[:, bank, :], ALU.add).then_inc(ring_read, 1)
                    if step == "w_split":
                        dve.wait_ge(w_hi_done, index + 1)
                        dve.tensor_tensor(w_lo[:, index, :], x[:, index, :], w_hi[:, index, :].bitcast(FP32),
                                          ALU.subtract).then_inc(w_lo_done, 1)

            loop(dve, body)

        @block.tensor
        def _(pe):
            pe.wait_ge(ones_set, TURN)

            def body(turn, steps, kind):
                base = slots_before(turn, kind)
                for step, index, k, slot in steps:
                    unit = turn * TURN_UNITS + index
                    bank = (parity(kind) + slot) % 2

                    def free():
                        if not (kind == "start" and slot < 2):
                            pe.wait_ge(ring_read, base + slot - 1)

                    if step == "max":
                        nb, c, i, t = index // CHUNKS % TURN, index % CHUNKS, k // TILES, k % TILES
                        turns = turn + index // TURN_CHUNKS + 1
                        if c == 0 and k == 0:
                            pe.wait_ge(qk_loaded[nb], turns * (2 * PLANES * 16))
                        if c == 1 and k == 0:
                            pe.wait_ge(queries_loaded[nb], turns * ((CHUNKS - 1) * PLANES * 16))
                        free()
                        nc.tensor.matmul(ring[:, bank, :], qk[0:AT_MAX, nb, c, i, t * P:(t + 1) * P],
                                         qk[0:AT_MAX, nb, CHUNKS, i, :], start=True, stop=True).then_inc(ring_written, 1)
                    if step == "max_turn":
                        if kind == "start":
                            pe.wait_ge(ident_loaded, 16)
                        pe.wait_ge(max_lo_done, turn * TURN_CHUNKS + index + 1)
                        free()
                        for t in range(TILES):
                            last_one = nc.tensor.transpose(ring[0:2 * HEADS, bank, t * P:(t + 1) * P],
                                                           max_parts[:, t].bitcast(FP32).rearrange("p a h -> p (a h)"),
                                                           ident[:])
                        last_one.then_inc(ring_written, 1)
                    if step == "scores":
                        g = index // UNITS
                        nb, c = g // CHUNKS % TURN, g % CHUNKS
                        i, half = index % UNITS // HALVES, index % HALVES
                        if index % UNITS == 0:
                            pe.wait_ge(rows_loaded, (turn * TURN_CHUNKS + g + 1) * 32)
                        wait(pe, exp_done, unit - 1)
                        for kc in range(2):
                            at = (half * 2 + kc) * P
                            last_one = nc.tensor.matmul(scores[:, index % 2, kc, :],
                                                        qk[0:AT_MAX + 2, nb, CHUNKS, i, at:at + P],
                                                        qk[0:AT_MAX + 2, nb, c, i, :], start=True, stop=True)
                        last_one.then_inc(scores_done, 1)
                    if step == "value":
                        g = index // UNITS
                        nb, i, half = g // CHUNKS, index % UNITS // HALVES, index % HALVES
                        pair = index // PAIR
                        if k == 0:
                            if index % (UNITS * CHUNKS) == 0:
                                pe.wait_ge(v_loaded[nb], (turn + 1) * 16)
                            if index % PAIR == 0:
                                wait(pe, joined, (turn * (TURN_UNITS // PAIR) + pair - 1) * 2)
                            wait_lo(pe, turn, index)
                        at = i * VW
                        values = v[:, nb, half * 2 + k, at:at + VW]
                        ph, pl = p_hi[:, index % RING, k, :], p_lo[:, index % RING, k, :]
                        begins, ends = index % PAIR == 0 and k == 0, index % PAIR == PAIR - 1 and k == 1
                        nc.tensor.matmul(out_t[:, pair % 2, :], values[:, 0:P], ph, start=begins, stop=False)
                        nc.tensor.matmul(out_t[0:P // 2, pair % 2, :], values[:, P:VW], ph, start=False, stop=False)
                        last_one = nc.tensor.matmul(out_t[:, pair % 2, :], values[:, 0:P], pl, start=False, stop=ends)
                        if k == 1:
                            last_one.then_inc(pv_done, 1)
                    if step == "out":
                        if k == 0:
                            pe.wait_ge(w_lo_done, CHUNKS)
                            pe.wait_ge(o_lo_done, (turn * TURN + index) * CHUNKS)
                        free()
                        for c in range(CHUNKS):
                            for j, (oo, ww) in enumerate(((o_hi, w_hi), (o_hi, w_lo), (o_lo, w_hi))):
                                last_one = nc.tensor.matmul(ring[:, bank, :], oo[:, c, k * P:(k + 1) * P],
                                                            ww[:, c, :], start=c == 0 and j == 0,
                                                            stop=c == CHUNKS - 1 and j == 2)
                        last_one.then_inc(ring_written, 1)

            loop(pe, body)




def macaron_layer(nc, ident, cos, sin, x, w_q, w_k, w_v, w_o, w_gate, w_up, w_down, out):
    seqs, seq, hidden = x.shape
    heads = w_k.shape[1] // HEAD
    chunks = w_q.shape[1] // P

    def scratch(name, shape):
        return nc.dram_tensor(name, shape, FP32, kind="Internal").ap()

    tokens_in, tokens_out = (a.rearrange("b s n -> (b s) n") for a in (x, out))
    after_ffn = scratch("after_ffn", (seqs * seq, hidden))
    after_attention = scratch("after_attention", (seqs * seq, hidden))
    qk_hi = scratch("qk_hi", (seqs, P, chunks + 1, seq))
    qk_lo = scratch("qk_lo", (seqs, P, chunks + 1, seq))
    values = scratch("values", (seqs, P, seq // P, heads * 3 * (P // 2)))

    ffn_phase(nc, ident, tokens_in, after_ffn, w_gate, w_up, w_down, "ffn1")
    qkv_phase(nc, ident, cos, sin, after_ffn, w_q, w_k, w_v, qk_hi, qk_lo, values, seq)
    attention_phase(nc, ident, qk_hi, qk_lo, values, w_o, after_ffn, after_attention, seq)
    ffn_phase(nc, ident, after_attention, tokens_out, w_gate, w_up, w_down, "ffn2")


def rotation_tables(seq, query_columns, key_columns):
    half = HEAD // 2
    freqs = (1.0 / np.float32(10000.0) ** (np.arange(half, dtype=np.float32) / np.float32(half))).astype(np.float32)
    angles = np.arange(seq, dtype=np.float32)[:, None] * freqs[None, :]
    cos = np.repeat(np.cos(angles), 2, axis=1)
    sin = np.repeat(np.sin(angles), 2, axis=1)
    sin[:, 0::2] *= -1.0
    scale = np.ones((1, query_columns + key_columns), np.float32)
    scale[:, :query_columns] = HEAD ** -0.5
    copies = (query_columns + key_columns) // HEAD
    return [(np.tile(a, (1, copies)) * scale).astype(np.float32) for a in (cos, sin)]


_INS = ["L0_attn_x", "L0_attn_W_q", "L0_attn_W_k", "L0_attn_W_v", "L0_attn_W_o",
        "L0_ffn_w_gate", "L0_ffn_w_up", "L0_ffn_w_down"]


def kernel(**inputs):
    import concourse.bacc as _bacc
    from concourse.bass_utils import run_bass_kernel_spmd as _run

    nc = _bacc.Bacc("TRN2", target_bir_lowering=False, num_devices=1)
    seq = inputs["L0_attn_x"].shape[1]
    cos, sin = rotation_tables(seq, inputs["L0_attn_W_q"].shape[1], inputs["L0_attn_W_k"].shape[1])
    arrays = {"identity": np.eye(P, dtype=np.float32), "cosines": cos, "sines": sin}
    arrays.update({name: np.ascontiguousarray(inputs[name]) for name in _INS})
    args = [nc.dram_tensor(n, a.shape, mybir.dt.from_np(a.dtype), kind="ExternalInput").ap() for n, a in arrays.items()]
    out = nc.dram_tensor("out", inputs["L0_attn_x"].shape, FP32, kind="ExternalOutput").ap()
    macaron_layer(nc, *args, out)
    return _run(nc, [arrays], core_ids=[0]).results[0]["out"]
```
